# Optimizing a Trainium2 kernel written in Bass

```python
import numpy as np
import jax
import jax.numpy as jnp

def _softmax(x, axis=-1):
    return jax.nn.softmax(x, axis=axis)

def _gelu(x):
    return jax.nn.gelu(x, approximate=True)

def _silu(x):
    return jax.nn.silu(x)

def _sigmoid(x):
    return jax.nn.sigmoid(x)

def _layernorm(x, axis=-1, eps=1e-05):
    m = jnp.mean(x, axis=axis, keepdims=True)
    v = jnp.var(x, axis=axis, keepdims=True)
    return (x - m) / jnp.sqrt(v + eps)

def _scatter_add(tgt, idx, src, axis=0):
    return tgt.at[idx].add(src)

def _segment_sum(src, seg, n):
    return jax.ops.segment_sum(src, seg, n)
kernel_name = 'mk_recurrent_d1_jaxref_r8_056844'

def setup_inputs(seed: int=0):
    np.random.seed(seed)
    _w = jnp.asarray

    def _L0_attn_setup():
        import math
        import jax, jax.numpy as jnp
        import numpy as np
        B, T, D_MODEL = (4, 256, 128)
        H, HD = (16, 64)
        NF = 128
        EPS = 1e-06
        INV_SQRT_NF = 1.0 / math.sqrt(NF)

        def make_orf(key, head_dim, n_features, dtype=jnp.float32):
            n_blocks = math.ceil(n_features / head_dim)
            keys = jax.random.split(key, n_blocks)
            blocks = []
            for k in keys:
                g = jax.random.normal(k, (head_dim, head_dim), dtype)
                qm, _ = jnp.linalg.qr(g)
                blocks.append(qm)
            W = jnp.concatenate(blocks, axis=1)[:, :n_features]
            return W * jnp.asarray(math.sqrt(head_dim), dtype)

        def _favor_plus(x, W):
            sq = 0.5 * jnp.sum(x * x, axis=-1, keepdims=True)
            return jnp.exp(x @ W - sq) * INV_SQRT_NF

        def _causal_linear_attention(qp, kp, v):
            Bb, Hh = (qp.shape[0], qp.shape[1])

            def step(carry, qkv):
                S, z = carry
                q_t, k_t, v_t = qkv
                S = S + jnp.einsum('bhd,bhe->bhde', k_t, v_t)
                z = z + k_t
                num = jnp.einsum('bhd,bhde->bhe', q_t, S)
                den = jnp.einsum('bhd,bhd->bh', q_t, z) + EPS
                return ((S, z), num / den[..., None])
            S0 = jnp.zeros((Bb, Hh, NF, HD), qp.dtype)
            z0 = jnp.zeros((Bb, Hh, NF), qp.dtype)
            xs = (jnp.moveaxis(qp, 2, 0), jnp.moveaxis(kp, 2, 0), jnp.moveaxis(v, 2, 0))
            _, ys = jax.lax.scan(step, (S0, z0), xs)
            return jnp.moveaxis(ys, 0, 2)
        key = jax.random.key(seed)
        k0, k1, k2, k3, k4, k5 = jax.random.split(key, 6)
        s = 1.0 / math.sqrt(D_MODEL)
        x = jax.random.normal(k0, (B, T, D_MODEL), jnp.float32)
        Wq = jax.random.uniform(k1, (D_MODEL, H * HD), jnp.float32, -s, s)
        Wk = jax.random.uniform(k2, (D_MODEL, H * HD), jnp.float32, -s, s)
        Wv = jax.random.uniform(k3, (D_MODEL, H * HD), jnp.float32, -s, s)
        Wo = jax.random.uniform(k4, (H * HD, D_MODEL), jnp.float32, -s, s)
        W_feat = make_orf(k5, HD, NF)
        return {'x': x, 'Wq': Wq, 'Wk': Wk, 'Wv': Wv, 'Wo': Wo, 'W_feat': W_feat}
    _L0_attn_in = _L0_attn_setup()

    def _L0_ffn_setup():
        import jax, jax.numpy as jnp
        import numpy as np
        B, T, C = (2, 64, 128)
        I = 512
        E = 8
        K = 2
        key = jax.random.key(seed)
        ks = jax.random.split(key, 8)
        s = 0.02
        return {'x': jax.random.normal(ks[0], (B, T, C), jnp.float32), 'Wr1': jax.random.normal(ks[1], (C, C // 4), jnp.float32) * s, 'br1': jnp.zeros((C // 4,), jnp.float32), 'Wr2': jax.random.normal(ks[2], (C // 4, E), jnp.float32) * s, 'br2': jnp.zeros((E,), jnp.float32), 'Ws1': jax.random.normal(ks[3], (C, I), jnp.float32) * s, 'bs1': jnp.zeros((I,), jnp.float32), 'Ws2': jax.random.normal(ks[4], (I, C), jnp.float32) * s, 'bs2': jnp.zeros((C,), jnp.float32), 'We1': jax.random.normal(ks[5], (E, C, I), jnp.float32) * s, 'be1': jnp.zeros((E, I), jnp.float32), 'We2': jax.random.normal(ks[6], (E, I, C), jnp.float32) * s, 'be2': jnp.zeros((E, C), jnp.float32)}
    _L0_ffn_in = _L0_ffn_setup()
    _d = {'L0_attn_x': _L0_attn_in['x'], 'L0_attn_Wq': _L0_attn_in['Wq'], 'L0_attn_Wk': _L0_attn_in['Wk'], 'L0_attn_Wv': _L0_attn_in['Wv'], 'L0_attn_Wo': _L0_attn_in['Wo'], 'L0_attn_W_feat': _L0_attn_in['W_feat'], 'L0_ffn_Wr1': _L0_ffn_in['Wr1'], 'L0_ffn_br1': _L0_ffn_in['br1'], 'L0_ffn_Wr2': _L0_ffn_in['Wr2'], 'L0_ffn_br2': _L0_ffn_in['br2'], 'L0_ffn_Ws1': _L0_ffn_in['Ws1'], 'L0_ffn_bs1': _L0_ffn_in['bs1'], 'L0_ffn_Ws2': _L0_ffn_in['Ws2'], 'L0_ffn_bs2': _L0_ffn_in['bs2'], 'L0_ffn_We1': _L0_ffn_in['We1'], 'L0_ffn_be1': _L0_ffn_in['be1'], 'L0_ffn_We2': _L0_ffn_in['We2'], 'L0_ffn_be2': _L0_ffn_in['be2']}
    _x0 = _d['L0_attn_x']
    _d['L0_attn_x'] = jax.random.normal(jax.random.fold_in(jax.random.key(seed), 1), (1, 2048, 128), dtype=_x0.dtype)
    del _x0
    return _d

def reference(L0_attn_x, L0_attn_Wq, L0_attn_Wk, L0_attn_Wv, L0_attn_Wo, L0_attn_W_feat, L0_ffn_Wr1, L0_ffn_br1, L0_ffn_Wr2, L0_ffn_br2, L0_ffn_Ws1, L0_ffn_bs1, L0_ffn_Ws2, L0_ffn_bs2, L0_ffn_We1, L0_ffn_be1, L0_ffn_We2, L0_ffn_be2):

    def _L0_attn_ref(x, Wq, Wk, Wv, Wo, W_feat):
        import math
        import jax, jax.numpy as jnp
        import numpy as np
        B, T, D_MODEL = (4, 256, 128)
        H, HD = (16, 64)
        NF = 128
        EPS = 1e-06
        INV_SQRT_NF = 1.0 / math.sqrt(NF)

        def make_orf(key, head_dim, n_features, dtype=jnp.float32):
            n_blocks = math.ceil(n_features / head_dim)
            keys = jax.random.split(key, n_blocks)
            blocks = []
            for k in keys:
                g = jax.random.normal(k, (head_dim, head_dim), dtype)
                qm, _ = jnp.linalg.qr(g)
                blocks.append(qm)
            W = jnp.concatenate(blocks, axis=1)[:, :n_features]
            return W * jnp.asarray(math.sqrt(head_dim), dtype)

        def _favor_plus(x, W):
            sq = 0.5 * jnp.sum(x * x, axis=-1, keepdims=True)
            return jnp.exp(x @ W - sq) * INV_SQRT_NF

        def _causal_linear_attention(qp, kp, v):
            Bb, Hh = (qp.shape[0], qp.shape[1])

            def step(carry, qkv):
                S, z = carry
                q_t, k_t, v_t = qkv
                S = S + jnp.einsum('bhd,bhe->bhde', k_t, v_t)
                z = z + k_t
                num = jnp.einsum('bhd,bhde->bhe', q_t, S)
                den = jnp.einsum('bhd,bhd->bh', q_t, z) + EPS
                return ((S, z), num / den[..., None])
            S0 = jnp.zeros((Bb, Hh, NF, HD), qp.dtype)
            z0 = jnp.zeros((Bb, Hh, NF), qp.dtype)
            xs = (jnp.moveaxis(qp, 2, 0), jnp.moveaxis(kp, 2, 0), jnp.moveaxis(v, 2, 0))
            _, ys = jax.lax.scan(step, (S0, z0), xs)
            return jnp.moveaxis(ys, 0, 2)
        Bb, Tt, _ = x.shape

        def heads(W):
            return (x @ W).reshape(Bb, Tt, H, HD).transpose(0, 2, 1, 3)
        q, k, v = (heads(Wq), heads(Wk), heads(Wv))
        qp = _favor_plus(q, W_feat)
        kp = _favor_plus(k, W_feat)
        y = _causal_linear_attention(qp, kp, v)
        y = y.transpose(0, 2, 1, 3).reshape(Bb, Tt, H * HD)
        return y @ Wo

    def _L0_ffn_ref(x, Wr1, br1, Wr2, br2, Ws1, bs1, Ws2, bs2, We1, be1, We2, be2):
        import jax, jax.numpy as jnp
        import numpy as np
        B, T, C = (2, 64, 128)
        I = 512
        E = 8
        K = 2
        Bb, Tt, Cc = x.shape
        xf = x.reshape(-1, Cc)
        logits = jax.nn.relu(xf @ Wr1 + br1) @ Wr2 + br2
        gates = jax.nn.softmax(logits, axis=-1)
        tg, ti = jax.lax.top_k(gates, K)
        tg = jax.nn.softmax(tg / K, axis=-1)
        out = jax.nn.silu(xf @ Ws1 + bs1) @ Ws2 + bs2
        for e in range(E):
            h = jax.nn.silu(xf @ We1[e] + be1[e]) @ We2[e] + be2[e]
            w = jnp.sum(tg * (ti == e), axis=-1)
            out = out + w[:, None] * h
        return out.reshape(Bb, Tt, Cc)
    x = L0_attn_x
    xn = _layernorm(x, axis=-1)
    s = _L0_attn_ref(xn, L0_attn_Wq, L0_attn_Wk, L0_attn_Wv, L0_attn_Wo, L0_attn_W_feat)
    g = _silu(_L0_ffn_ref(xn, L0_ffn_Wr1, L0_ffn_br1, L0_ffn_Wr2, L0_ffn_br2, L0_ffn_Ws1, L0_ffn_bs1, L0_ffn_Ws2, L0_ffn_bs2, L0_ffn_We1, L0_ffn_be1, L0_ffn_We2, L0_ffn_be2))
    x = x + s * g
    return x

_drawn_inputs = setup_inputs


def setup_inputs(seed=0):
    import zlib

    import numpy as np

    out = dict(_drawn_inputs(seed))
    spreads = {'L0_ffn_br1': (0.0, 0.8),
     'L0_ffn_br2': (0.0, 0.37),
     'L0_ffn_bs1': (0.0, 0.8),
     'L0_ffn_bs2': (0.0, 0.37),
     'L0_ffn_be1': (0.0, 0.8),
     'L0_ffn_be2': (0.0, 0.525)}
    factors = {'L0_ffn_Wr1': 8.0,
     'L0_ffn_Wr2': 4.88,
     'L0_ffn_Ws1': 4.782,
     'L0_ffn_Ws2': 4.395,
     'L0_ffn_We1': 6.772,
     'L0_ffn_We2': 6.24}
    for name, (base, spread) in spreads.items():
        noise = np.random.default_rng([zlib.crc32(name.encode()), seed]).standard_normal(out[name].shape)
        drawn = base * np.exp(spread * noise) if base else spread * noise
        out[name] = jnp.asarray(drawn.astype(out[name].dtype))
    for name, factor in factors.items():
        out[name] = (out[name] * factor).astype(out[name].dtype)
    return out
```

```python
from contextlib import ExitStack

import concourse.bass as bass
import concourse.mybir as mybir

F32 = mybir.dt.float32
F32R = mybir.dt.float32r
U32 = mybir.dt.uint32
ALU = mybir.AluOpType
ACT = mybir.ActivationFunctionType
AX = mybir.AxisListType

P = 128
HD = 64
NF = 128
HG = 4
NCHUNK = 16
UNIT = 4
TU = UNIT * P
EV = HD + 1
LN_EPS = 1e-5
EPS = 1e-6


def build(nc, x, Wq, Wk, Wv, Wo, W_feat, Wr1, br1, Wr2, br2, Ws1, bs1, Ws2, bs2, We1, be1, We2, be2, out):
    T, C = x.shape[1], x.shape[2]
    H = Wq.shape[1] // HD
    NG = H // HG
    GW = HG * HD
    NU = NCHUNK // UNIT
    R = Wr1.shape[1]
    E, _, I = We1.shape
    IB = I // P
    NX = E + 1
    assert T == NCHUNK * P and C == P and W_feat.shape == (HD, NF)

    x_d = x.rearrange("a (n p) c -> p (a n) c", p=P)
    out_d = out.rearrange("a (n p) c -> p (a n) c", p=P)

    with ExitStack() as ctx:
        def sb(name, shape, dt=F32):
            return ctx.enter_context(nc.sbuf_tensor(name, shape, dt))

        def sem(name):
            return ctx.enter_context(nc.semaphore(name))

        x_sb = sb("x_sb", [P, NCHUNK, C])
        xn = sb("xn", [P, NCHUNK, C])
        xT_hi = sb("xT_hi", [P, T], F32R)
        xT_lo = sb("xT_lo", [P, T], F32R)
        ident = sb("ident", [P, P])
        stats = sb("stats", [P, NCHUNK, 6])
        mean_var = sb("mean_var", [P, NCHUNK, 2])
        rstd = sb("rstd", [P, NCHUNK])
        minus_half = sb("minus_half", [P, NCHUNK])
        w_raw = sb("w_raw", [P, 3, GW])
        w_hi = sb("w_hi", [P, 3, GW], F32R)
        w_lo = sb("w_lo", [P, 3, GW], F32R)
        wo = sb("wo", [P, H * HD // P, C])
        wf_q = sb("wf_q", [P, 2, NF])
        stack = sb("stack", [P, 2, 2, TU])
        phi = sb("phi", [P, 2, 2, HG, TU])
        v1 = sb("v1", [P, 2, UNIT, HG, EV])
        causal = sb("causal", [P, HG, P])
        probs = sb("probs", [P, HG, P])
        k_tok = sb("k_tok", [P, HG, NF])
        state = sb("state", [P, 2, HG, EV])
        den = sb("den", [P, HG])
        y = sb("y", [P, HG, HD])
        yT = sb("yT", [P, 2, P])
        s_sum = sb("s_sum", [P, NCHUNK, C])
        wr1 = sb("wr1", [P, P])
        wr1_hi = sb("wr1_hi", [P, P], F32R)
        wr1_lo = sb("wr1_lo", [P, P], F32R)
        br1_c = sb("br1_c", [R, 1])
        wr2 = sb("wr2", [R + 1, E])
        hr = sb("hr", [R + 1, T])
        gate = sb("gate", [P, NCHUNK, E])
        row1 = sb("row1", [P, NCHUNK])
        row2 = sb("row2", [P, NCHUNK])
        top = sb("top", [P, NCHUNK, 8])
        top_at = sb("top_at", [P, NCHUNK, 8], U32)
        top_e = sb("top_e", [P, NCHUNK, 2])
        tp = sb("tp", [P, 2, NCHUNK])
        iota_e = sb("iota_e", [P, NCHUNK, E])
        wtok = sb("wtok", [P, NCHUNK, E])
        wtmp = sb("wtmp", [P, NCHUNK, E])
        wtokT = sb("wtokT", [P, P])
        be2_bd = sb("be2_bd", [P, NCHUNK, C])
        bs2_b = sb("bs2_b", [P, C])
        e1_raw = sb("e1_raw", [P, 2, I])
        e1_hi = sb("e1_hi", [P, NX, I], F32R)
        e1_lo = sb("e1_lo", [P, NX, I], F32R)
        e1_rows = sb("e1_rows", [P, P])
        e1_b = sb("e1_b", [P, NX, IB])
        e2 = sb("e2", [P, NX, IB, C])
        hid = [phi[:, k // 2, k % 2, :, :] for k in range(3)]
        acc = xn

        bank = [ctx.enter_context(nc.psum_tensor(f"bank{i}", [P, 512], F32)) for i in range(8)]
        PROJ, VY, FEAT, SCORE, KTOK, OUT, STATE = bank[0], bank[1], bank[2:4], bank[4], bank[5], bank[6], bank[7]

        x_in = [sem(f"x_in{i}") for i in range(NU)]
        w_in = [sem("wq_in"), sem("wk_in"), sem("wv_in")]
        wo_in, wf_in = sem("wo_in"), sem("wf_in")
        r_in, b_in, e2_in, bd_in = sem("r_in"), sem("b_in"), sem("e2_in"), sem("bd_in")
        e1_in = [sem("e1_in0"), sem("e1_in1")]
        out_done = sem("out_done")
        consts_done = sem("consts_done")
        bd_zero = sem("bd_zero")
        half_done = sem("half_done")
        eps_done, rstd_done = sem("eps_done"), sem("rstd_done")
        r_split = sem("r_split")
        w_hi_done = [sem("wq_hi_done"), sem("wk_hi_done"), sem("wv_hi_done")]
        w_split = [sem("wq_split"), sem("wk_split"), sem("wv_split")]
        hi_done = sem("hi_done")
        e1_split = sem("e1_split")
        var_done, xn_done = sem("var_done"), sem("xn_done")
        xt_ready, xhi_done, xlo_done = sem("xt_ready"), sem("xhi_done"), sem("xlo_done")
        dve = sem("dve")
        rh_ready, rh_done, lg_ready = sem("rh_ready"), sem("rh_done"), sem("lg_ready")
        lg_done, ex_done, d_done, e2x_done = sem("lg_done"), sem("ex_done"), sem("d_done"), sem("e2x_done")
        w_done, wt_ready, wt_done = sem("w_done"), sem("wt_ready"), sem("wt_done")
        proj_ready, q_copied, q_squared = sem("proj_ready"), sem("q_copied"), sem("q_squared")
        feat_ready, phi_done = sem("feat_ready"), sem("phi_done")
        score_ready, masked = sem("score_ready"), sem("masked")
        ktok_ready, ktok_done = sem("ktok_ready"), sem("ktok_done")
        outp_ready, y_done = sem("outp_ready"), sem("y_done")
        vy_ready, v_done, yt_ready, yt_done = sem("vy_ready"), sem("v_done"), sem("yt_ready"), sem("yt_done")
        den_done, m_done, lgs_done = sem("den_done"), sem("m_done"), sem("lgs_done")
        st_ready, st_done, s_added = sem("st_ready"), sem("st_done"), sem("s_added")
        h_ready, h_done = sem("h_ready"), sem("h_done")
        o_ready, o_done = sem("o_ready"), sem("o_done")
        g_done, res_done = sem("g_done"), sem("res_done")

        block = ctx.enter_context(nc.Block())

        LAST = NG * NCHUNK

        FEAT_AHEAD, PROJ_AHEAD = 4, 5

        def over_groups(eng, step, after, between=None):
            for n in range(-PROJ_AHEAD, 0):
                step(0, n)
            with eng.Fori(0, NG - 1) as g:
                for i in range(NCHUNK):
                    step(g, i)
                after(g)
            for i in range(NCHUNK):
                step(NG - 1, i)
                if between is not None:
                    between(i)
            after(NG - 1)

        def ahead(g, i, by):
            return i + by >= 0 and not (isinstance(g, int) and g * NCHUNK + i + by >= LAST)

        RESPLIT = {9: (0, 14), 11: (1, 16), 12: (2, 16)}

        @block.sync
        def _(sp):
            for u in range(NU):
                sp.dma_start(x_sb[:, u * UNIT:(u + 1) * UNIT, :], x_d[:, u * UNIT:(u + 1) * UNIT, :]).then_inc(x_in[u], 16)
            for j, (src, arrived) in enumerate(((Wq, w_in[0]), (Wk, w_in[1]), (Wv, w_in[2]))):
                sp.dma_start(w_raw[:, j, :], src[:, 0:GW]).then_inc(arrived, 16)
            sp.wait_ge(bd_zero, 1)
            sp.dma_start(wr1[:, 0:R], Wr1).then_inc(r_in, 16)
            sp.dma_start(br1_c[:, :], br1.rearrange("(r a) -> r a", a=1)).then_inc(r_in, 16)
            sp.dma_start(wr2[0:R, :], Wr2).then_inc(r_in, 16)
            sp.dma_start(wr2[R:R + 1, :], br2.rearrange("(a e) -> a e", a=1)).then_inc(r_in, 16)
            sp.dma_start(e1_rows[0:IB, :], bs1.rearrange("(b p) -> b p", p=P)).then_inc(b_in, 16)
            sp.dma_start(e1_rows[IB:NX * IB, :], be1.rearrange("e (b p) -> (e b) p", p=P)).then_inc(b_in, 16)
            sp.dma_start(wf_q[0:HD, 0, :], W_feat).then_inc(wf_in, 16)
            sp.dma_start(wf_q[HD:P, 1, :], W_feat).then_inc(wf_in, 16)
            sp.dma_start(wo[:, :, :], Wo.rearrange("(b p) c -> p b c", p=P)).then_inc(wo_in, 16)
            for e in range(NX):
                if e >= 2:
                    sp.wait_ge(e1_split, e - 1)
                sp.dma_start(e1_raw[:, e % 2, :], Ws1 if e == 0 else We1[e - 1]).then_inc(e1_in[e % 2], 16)
            sp.dma_start(bs2_b[:, :], bs2.rearrange("(a c) -> a c", a=1).broadcast_to([P, C])).then_inc(b_in, 16)
            sp.dma_start(e2[:, 0, :, :], Ws2.rearrange("(b p) c -> p b c", p=P)).then_inc(e2_in, 16)
            sp.dma_start(e2[:, 1:NX, :, :], We2.rearrange("e (b p) c -> p e b c", p=P)).then_inc(e2_in, 16)
            sp.wait_ge(bd_zero, 2)
            for n in range(NCHUNK):
                sp.dma_start(be2_bd[n * E:(n + 1) * E, n, :], be2).then_inc(bd_in, 16)
            with sp.Fori(0, NG - 1) as g:
                for j, src in enumerate((Wq, Wk, Wv)):
                    sp.wait_ge(w_split[j], g + 1)
                    sp.dma_start(w_raw[:, j, :], src[:, bass.ds((g + 1) * GW, GW)]).then_inc(w_in[j], 16)
            for u in range(NU):
                sp.wait_ge(res_done, u + 1)
                sp.dma_start(out_d[:, u * UNIT:(u + 1) * UNIT, :], x_sb[:, u * UNIT:(u + 1) * UNIT, :]).then_inc(out_done, 16)
            sp.wait_ge(out_done, 16 * NU)

        @block.gpsimd
        def _(pool):
            nc.gpsimd.memset(ident[:, :], 0.0).then_inc(consts_done, 1)
            nc.gpsimd.memset(minus_half[:, :], -0.5)
            pool.wait_ge(consts_done, 1)
            nc.gpsimd.affine_select(out=ident[:, :], in_=ident[:, :], compare_op=ALU.not_equal, fill=1.0, base=0,
                                    pattern=[[-1, P]], channel_multiplier=1).then_inc(consts_done, 1)
            nc.gpsimd.memset(e1_rows[:, :], 0.0)
            nc.gpsimd.memset(wr1[:, :], 0.0).then_inc(bd_zero, 1)
            nc.gpsimd.iota(iota_e[:, :, :], pattern=[[0, NCHUNK], [1, E]], base=0, channel_multiplier=0,
                           allow_small_or_imprecise_dtypes=True)
            nc.gpsimd.memset(causal[:, :, :], 1.0).then_inc(consts_done, 1)
            pool.wait_ge(consts_done, 3)
            nc.gpsimd.affine_select(out=causal[:, :, :], in_=causal[:, :, :], compare_op=ALU.is_ge, fill=0.0, base=0,
                                    pattern=[[0, HG], [1, P]], channel_multiplier=-1).then_inc(consts_done, 1)
            pool.wait_ge(var_done, 1)
            nc.gpsimd.tensor_scalar(rstd[:, :], mean_var[:, :, 1], LN_EPS, None, ALU.add).then_inc(eps_done, 1)
            pool.wait_ge(eps_done, 1)
            nc.gpsimd.tensor_tensor(rstd[:, :], rstd[:, :], minus_half[:, :], ALU.pow).then_inc(rstd_done, 1)

            splits = [0]

            def split(hi, lo, raw):
                nc.gpsimd.tensor_copy(hi, raw).then_inc(hi_done, 1)
                splits[0] += 1
                pool.wait_ge(hi_done, splits[0])
                return nc.gpsimd.tensor_tensor(lo, raw, hi.bitcast(F32), ALU.subtract)

            pool.wait_ge(r_in, 64)
            split(wr1_hi[:, :], wr1_lo[:, :], wr1[:, :]).then_inc(r_split, 1)
            nc.gpsimd.memset(v1[:, :, :, :, :], 1.0).then_inc(consts_done, 1)
            nc.gpsimd.memset(s_sum[:, :, :], 0.0).then_inc(consts_done, 1)
            nc.gpsimd.memset(be2_bd[:, :, :], 0.0).then_inc(bd_zero, 1)
            for e in range(NX):
                pool.wait_ge(e1_in[e % 2], 16 * (e // 2 + 1))
                split(e1_hi[:, e, :], e1_lo[:, e, :], e1_raw[:, e % 2, :]).then_inc(e1_split, 1)

        @block.tensor
        def _(pe):
            def mm3(dst, l_hi, l_lo, r_hi, r_lo, start=True, stop=True):
                nc.tensor.matmul(dst, l_hi, r_hi, start=start, stop=False)
                nc.tensor.matmul(dst, l_hi, r_lo, start=False, stop=False)
                return nc.tensor.matmul(dst, l_lo, r_hi, start=False, stop=stop)

            pe.wait_ge(consts_done, 2)
            for u in range(NU):
                pe.wait_ge(xn_done, u + 1)
                for c in range(UNIT):
                    last = nc.tensor.transpose(bank[u][:, c * P:(c + 1) * P], xn[:, u * UNIT + c, :], ident[:, :])
                last.then_inc(xt_ready, 1)

            pe.wait_ge(r_split, 1)
            pe.wait_ge(half_done, 1)
            for u in range(NU):
                pe.wait_ge(xlo_done, u + 1)
                mm3(bank[4 + u][:, :], wr1_hi[:, :], wr1_lo[:, :], xT_hi[:, u * TU:(u + 1) * TU],
                    xT_lo[:, u * TU:(u + 1) * TU]).then_inc(rh_ready, 1)
            for n in range(NCHUNK):
                if n % UNIT == 0:
                    pe.wait_ge(rh_done, n // UNIT + 1)
                last = nc.tensor.matmul(bank[0][:, n * E:(n + 1) * E],
                                        hr[:, n * P:(n + 1) * P], wr2[:, :], start=True, stop=True)
            last.then_inc(lg_ready, 1)
            pe.wait_ge(lg_done, 1)

            def step(g, i):
                n = g * NCHUNK + i
                u, c = (i // UNIT) % 2, i % UNIT
                attends = i >= 0
                if attends:
                    if c == 0:
                        pe.wait_ge(phi_done, n * 2 + 2 * UNIT)
                    for h in range(HG):
                        last = nc.tensor.matmul(SCORE[:, h * P:(h + 1) * P], phi[:, u, 1, h, c * P:(c + 1) * P],
                                                phi[:, u, 0, h, c * P:(c + 1) * P], start=True, stop=True)
                    last.then_inc(score_ready, 1)
                    if i < NCHUNK - 1:
                        for h in range(HG):
                            last = nc.tensor.transpose(KTOK[:, h * P:(h + 1) * P],
                                                       phi[:, u, 1, h, c * P:(c + 1) * P], ident[:, :])
                        last.then_inc(ktok_ready, 1)

                def feature(h):
                    j = n + FEAT_AHEAD
                    s = (i + FEAT_AHEAD) % 2
                    if h == 0:
                        pe.wait_ge(q_squared, j + 1)
                    if not isinstance(j, int) or j > 0:
                        pe.wait_ge(phi_done, j * 2 + (h - 1))
                    nc.tensor.matmul(FEAT[h][:, :], wf_q[:, h, :], stack[:, s, h, :],
                                     start=True, stop=True).then_inc(feat_ready, 1)

                if ahead(g, i, FEAT_AHEAD):
                    if i == -FEAT_AHEAD:
                        pe.wait_ge(wf_in, 32)
                    feature(0)

                if attends and i > 0:
                    pe.wait_ge(st_done, g * (NCHUNK - 1) + i)
                    for h in range(HG):
                        nc.tensor.matmul(OUT[:, h * EV:(h + 1) * EV], phi[:, u, 0, h, c * P:(c + 1) * P],
                                         state[:, i % 2, h, :], start=(h == 0), stop=False, skip_group_check=True)

                if ahead(g, i, PROJ_AHEAD):
                    b = (i + PROJ_AHEAD) % UNIT
                    t0 = (i + PROJ_AHEAD) % NCHUNK // UNIT * TU
                    if i == -PROJ_AHEAD:
                        pe.wait_ge(xlo_done, NU)
                    if b == 0 and t0 == 0:
                        pe.wait_ge(w_split[0], g + (i + PROJ_AHEAD) // NCHUNK + 1)
                    if b == 2 and t0 == 0:
                        pe.wait_ge(w_split[1], g + (i + PROJ_AHEAD) // NCHUNK + 1)
                    if i > -PROJ_AHEAD:
                        pe.wait_ge(q_copied, n + PROJ_AHEAD)
                    cols = slice(b % 2 * P, b % 2 * P + P)
                    mm3(PROJ[:, :], w_hi[:, b // 2, cols], w_lo[:, b // 2, cols], xT_hi[:, t0:t0 + TU],
                        xT_lo[:, t0:t0 + TU]).then_inc(proj_ready, 1)

                if attends:
                    pe.wait_ge(masked, n + 1)
                    if c == 0:
                        pe.wait_ge(v_done, n + UNIT)
                    for h in range(HG):
                        last = nc.tensor.matmul(OUT[:, h * EV:(h + 1) * EV], probs[:, h, :], v1[:, u, c, h, :],
                                                start=(i == 0 and h == 0), stop=True, skip_group_check=True)
                    last.then_inc(outp_ready, 1)

                if ahead(g, i, FEAT_AHEAD):
                    feature(1)

                if attends and i < NCHUNK - 1:
                    pe.wait_ge(ktok_done, g * (NCHUNK - 1) + (i + 1))
                    for h in range(HG):
                        last = nc.tensor.matmul(STATE[:, h * EV:(h + 1) * EV], k_tok[:, h, :], v1[:, u, c, h, :],
                                                start=True, stop=True)
                    if i == 0:
                        last.then_inc(st_ready, 1)
                if attends and i > 0:
                    output(g, i - 1, STATE)

                if ahead(g, i, FEAT_AHEAD):
                    j = (i + FEAT_AHEAD) % NCHUNK
                    if j == 0:
                        pe.wait_ge(w_split[2], g + (i + FEAT_AHEAD) // NCHUNK + 1)
                    if i > -FEAT_AHEAD:
                        pe.wait_ge(v_done, n + FEAT_AHEAD)
                    last = mm3(VY[:, 0:GW], xT_hi[:, j * P:(j + 1) * P], xT_lo[:, j * P:(j + 1) * P],
                               w_hi[:, 2, :], w_lo[:, 2, :])
                    last.then_inc(vy_ready, 1)
                if attends:
                    pe.wait_ge(y_done, n + 1)
                    for p in range(2):
                        last = nc.tensor.transpose(VY[:, GW + p * P:GW + (p + 1) * P], y[:, 2 * p:2 * p + 2, :],
                                                   ident[:, :])
                    last.then_inc(yt_ready, 1)

            def output(g, i, dst):
                pe.wait_ge(yt_done, g * NCHUNK + (i + 1))
                for p in range(2):
                    last = nc.tensor.matmul(dst[:, 384:384 + C], yT[:, p, :], wo[:, bass.ds(g * 2 + p, 1), :],
                                            start=(p == 0), stop=(p == 1))
                last.then_inc(st_ready, 1)

            def after(g):
                output(g, NCHUNK - 1, OUT)

            pe.wait_ge(wo_in, 16)
            over_groups(pe, step, after)

            pe.wait_ge(w_done, 1)
            pe.wait_ge(b_in, 48)
            nc.tensor.transpose(bank[0][:, 0:P], wtok[:, :, :], ident[:, :])
            nc.tensor.transpose(bank[0][:, P:2 * P], e1_rows[:, :], ident[:, :]).then_inc(wt_ready, 1)
            pe.wait_ge(wt_done, 1)
            pe.wait_ge(e1_split, NX)
            pe.wait_ge(e2_in, 32)
            pe.wait_ge(bd_in, 16 * NCHUNK)

            with pe.Fori(0, NU) as u:
                tokens = bass.ds(u * TU, TU)

                def first(e):
                    for b in range(IB):
                        if e > 0:
                            pe.wait_ge(h_done, u * (NX * IB) + ((e - 1) * IB + b + 1))
                        cols = slice(b * P, (b + 1) * P)
                        mm3(bank[b][:, :], e1_hi[:, e, cols], e1_lo[:, e, cols], xT_hi[:, tokens],
                            xT_lo[:, tokens]).then_inc(h_ready, 1)

                def second(e):
                    pe.wait_ge(h_done, u * (NX * IB) + (e + 1) * IB)
                    if e in (1, 2):
                        pe.wait_ge(o_done, u * NX + 1)
                    elif e > 2:
                        pe.wait_ge(o_done, u * NX + (e - 2))
                    dst = bank[4 + e % 3]
                    if e == 0:
                        nc.tensor.matmul(dst[:, :], wtokT[:, :], be2_bd[:, bass.ds(u * UNIT, UNIT), :],
                                         start=True, stop=False, skip_group_check=True)
                    for c in range(UNIT):
                        for b in range(IB):
                            last = nc.tensor.matmul(dst[:, c * P:(c + 1) * P], hid[e % 3][:, b, c * P:(c + 1) * P],
                                                    e2[:, e, b, :], start=(e > 0 and b == 0), stop=(b == IB - 1),
                                                    skip_group_check=True)
                    last.then_inc(o_ready, 1)

                first(0)
                for e in range(1, NX):
                    first(e)
                    second(e - 1)
                second(NX - 1)
                pe.wait_ge(o_done, u * NX + (NX - 1))

        @block.scalar
        def _(act):
            for u in range(NU):
                act.wait_ge(xt_ready, u + 1)
                nc.scalar.copy(xT_hi[:, u * TU:(u + 1) * TU], bank[u][:, :]).then_inc(xhi_done, 1)
            for j in range(3):
                act.wait_ge(w_in[j], 16)
                nc.scalar.copy(w_hi[:, j, :], w_raw[:, j, :]).then_inc(w_hi_done[j], 1)
            act.wait_ge(r_in, 64)
            for u in range(NU):
                act.wait_ge(rh_ready, u + 1)
                nc.scalar.activation(hr[0:R, u * TU:(u + 1) * TU], bank[4 + u][0:R, :], ACT.Relu,
                                     bias=br1_c[:, :]).then_inc(rh_done, 1)

            def step(g, i):
                n = g * NCHUNK + i
                if i in RESPLIT and not isinstance(g, int):
                    j, slots = RESPLIT[i]
                    act.wait_ge(w_in[j], g * 16 + 32)
                    act.wait_ge(vy_ready if j == 2 else proj_ready, g * NCHUNK + slots)
                    nc.scalar.copy(w_hi[:, j, :], w_raw[:, j, :]).then_inc(w_hi_done[j], 1)
                if 0 <= i < NCHUNK - 1:
                    act.wait_ge(ktok_ready, g * (NCHUNK - 1) + (i + 1))
                    nc.scalar.copy(k_tok[:, :, :], KTOK[:, :]).then_inc(ktok_done, 1)

                def features(h):
                    b, u = i % UNIT, (i + FEAT_AHEAD) // UNIT % 2
                    act.wait_ge(feat_ready, n * 2 + (2 * FEAT_AHEAD + h + 1))
                    nc.scalar.activation(phi[:, u, b // 2, b % 2 * 2 + h, :], FEAT[h][:, :], ACT.Exp).then_inc(phi_done, 1)

                if ahead(g, i, FEAT_AHEAD):
                    features(0)
                if ahead(g, i, PROJ_AHEAD):
                    s = (i + PROJ_AHEAD) % 2
                    act.wait_ge(q_copied, n + PROJ_AHEAD + 1)
                    nc.scalar.activation(stack[HD:P, s, 0, :], stack[0:HD, s, 0, :], ACT.Square)
                    nc.scalar.activation(stack[0:HD, s, 1, :], stack[HD:P, s, 1, :], ACT.Square).then_inc(q_squared, 1)
                if ahead(g, i, FEAT_AHEAD):
                    features(1)
                    act.wait_ge(vy_ready, n + FEAT_AHEAD + 1)
                    if i >= 0:
                        act.wait_ge(yt_ready, n + 1)
                    if i == -FEAT_AHEAD:
                        act.wait_ge(consts_done, 5)
                    nc.scalar.copy(v1[:, (i + FEAT_AHEAD) // UNIT % 2, i % UNIT, :, 0:HD],
                                   VY[:, 0:GW].rearrange("p (h d) -> p h d", d=HD)).then_inc(v_done, 1)
                if i >= 0:
                    act.wait_ge(yt_ready, n + 1)
                    nc.scalar.copy(yT[:, :, :], VY[:, GW:2 * GW]).then_inc(yt_done, 1)

            def after(g):
                pass

            def between(i):
                if i == 2:
                    act.wait_ge(lgs_done, 1)
                    nc.scalar.activation(gate[:, :, :], gate[:, :, :], ACT.Exp).then_inc(ex_done, 1)
                if i == 5:
                    act.wait_ge(d_done, 1)
                    nc.scalar.activation(row2[:, :], row2[:, :], ACT.Exp, scale=0.5).then_inc(e2x_done, 1)

            over_groups(act, step, after, between)

            act.wait_ge(wt_ready, 1)
            nc.scalar.copy(wtokT[:, :], bank[0][:, 0:P])
            nc.scalar.copy(e1_b[:, :, :], bank[0][:, P:P + NX * IB]).then_inc(wt_done, 1)
            act.wait_ge(wt_done, 1)
            with act.Fori(0, NU) as u:
                for e in range(NX):
                    for b in range(IB):
                        act.wait_ge(h_ready, u * (NX * IB) + (e * IB + b + 1))
                        nc.scalar.activation(hid[e % 3][:, b, :], bank[b][:, :], ACT.Silu,
                                             bias=e1_b[:, e, b:b + 1]).then_inc(h_done, 1)
                act.wait_ge(o_done, u * NX + NX)
                part = acc[:, bass.ds(u * UNIT, UNIT), :]
                nc.scalar.activation(part, part, ACT.Silu).then_inc(g_done, 1)

        @block.vector
        def _(vec):
            chain = [0]

            def link(ins):
                chain[0] += 1
                ins.then_inc(dve, 1)
                vec.wait_ge(dve, chain[0])

            nc.vector.memset(wf_q[HD:P, 0, :], -0.5)
            nc.vector.memset(wf_q[0:HD, 1, :], -0.5)
            nc.vector.memset(hr[R:R + 1, :], 1.0).then_inc(half_done, 1)
            for u in range(NU):
                vec.wait_ge(x_in[u], 16)
                for n in range(u * UNIT, (u + 1) * UNIT):
                    last = nc.vector.bn_stats(stats[:, n, :], x_sb[:, n, :])
            link(last)
            for n in range(NCHUNK):
                last = nc.vector.bn_aggr(mean_var[:, n, :], stats[:, n, :])
            last.then_inc(var_done, 1)
            vec.wait_ge(var_done, 1)
            vec.wait_ge(rstd_done, 1)
            for n in range(NCHUNK):
                last = nc.vector.tensor_scalar(xn[:, n, :], x_sb[:, n, :], mean_var[:, n, 0:1], rstd[:, n:n + 1],
                                               ALU.subtract, ALU.mult)
                if n % UNIT == UNIT - 1:
                    last.then_inc(xn_done, 1)
            for u in range(NU):
                vec.wait_ge(xhi_done, u + 1)
                t = slice(u * TU, (u + 1) * TU)
                nc.vector.tensor_tensor(xT_lo[:, t], bank[u][:, :], xT_hi[:, t].bitcast(F32),
                                        ALU.subtract).then_inc(xlo_done, 1)
            for j in range(3):
                vec.wait_ge(w_hi_done[j], 1)
                nc.vector.tensor_tensor(w_lo[:, j, :], w_raw[:, j, :], w_hi[:, j, :].bitcast(F32),
                                        ALU.subtract).then_inc(w_split[j], 1)
            vec.wait_ge(lg_ready, 1)
            nc.vector.tensor_copy(gate[:, :, :], bank[0][:, 0:NCHUNK * E]).then_inc(lg_done, 1)

            def step(g, i):
                n = g * NCHUNK + i
                if i in RESPLIT and not isinstance(g, int):
                    j = RESPLIT[i][0]
                    vec.wait_ge(w_hi_done[j], g + 2)
                    nc.vector.tensor_tensor(w_lo[:, j, :], w_raw[:, j, :], w_hi[:, j, :].bitcast(F32),
                                            ALU.subtract).then_inc(w_split[j], 1)
                if i >= 0:
                    vec.wait_ge(score_ready, n + 1)
                    nc.vector.tensor_tensor(probs[:, :, :], SCORE[:, :].rearrange("p (h q) -> p h q", q=P),
                                            causal[:, :, :], ALU.mult).then_inc(masked, 1)
                if ahead(g, i, PROJ_AHEAD):
                    s = (i + PROJ_AHEAD) % 2
                    vec.wait_ge(proj_ready, n + PROJ_AHEAD + 1)
                    nc.vector.tensor_copy(stack[0:HD, s, 0, :], PROJ[0:HD, :])
                    nc.vector.tensor_copy(stack[HD:P, s, 1, :], PROJ[HD:P, :]).then_inc(q_copied, 1)
                if i >= 0:
                    vec.wait_ge(outp_ready, n + 1)
                    o = OUT[:, 0:HG * EV].rearrange("p (h e) -> p h e", e=EV)
                    nc.vector.tensor_scalar(den[:, :], o[:, :, HD], NF * EPS, None, ALU.add).then_inc(den_done, 1)
                    vec.wait_ge(den_done, n * 2 + 1)
                    nc.vector.reciprocal(den[:, :], den[:, :]).then_inc(den_done, 1)
                    vec.wait_ge(den_done, n * 2 + 2)
                    nc.vector.tensor_tensor(y[:, :, :], o[:, :, 0:HD], den[:, :].unsqueeze(2).to_broadcast([P, HG, HD]),
                                            ALU.mult).then_inc(y_done, 1)
                    vec.wait_ge(st_ready, g * (NCHUNK + 1) + (i + 1))
                    if i > 0:
                        gather(i - 1, STATE)
                    if i < NCHUNK - 1:
                        new, old = state[:, (i + 1) % 2, :, :], state[:, i % 2, :, :]
                        delta = STATE[:, 0:HG * EV].rearrange("p (h e) -> p h e", e=EV)
                        if i == 0:
                            nc.vector.tensor_copy(new, delta).then_inc(st_done, 1)
                        else:
                            vec.wait_ge(st_done, g * (NCHUNK - 1) + i)
                            nc.vector.tensor_tensor(new, delta, old, ALU.add).then_inc(st_done, 1)

            def gather(i, src):
                nc.vector.tensor_tensor(s_sum[:, i, :], src[:, 384:384 + C], s_sum[:, i, :], ALU.add).then_inc(s_added, 1)

            def after(g):
                vec.wait_ge(st_ready, g * (NCHUNK + 1) + (NCHUNK + 1))
                gather(NCHUNK - 1, OUT)

            def bc(a, k=E):
                return a.unsqueeze(2).to_broadcast([P, NCHUNK, k])

            def between(i):
                if i == 1:
                    vec.wait_ge(lg_done, 1)
                    link(nc.vector.tensor_reduce(row1[:, :], gate[:, :, :], AX.X, ALU.max))
                    nc.vector.tensor_tensor(gate[:, :, :], gate[:, :, :], bc(row1[:, :]), ALU.subtract).then_inc(lgs_done, 1)
                if i == 3:
                    vec.wait_ge(ex_done, 1)
                    link(nc.vector.tensor_reduce(row1[:, :], gate[:, :, :], AX.X, ALU.add))
                    link(nc.vector.reciprocal(row1[:, :], row1[:, :]))
                    link(nc.vector.tensor_tensor(gate[:, :, :], gate[:, :, :], bc(row1[:, :]), ALU.mult))
                    for n in range(NCHUNK):
                        last = nc.vector.max(top[:, n, :], gate[:, n, :])
                    link(last)
                    nc.vector.tensor_tensor(row2[:, :], top[:, :, 1], top[:, :, 0], ALU.subtract).then_inc(d_done, 1)
                if i == 4:
                    for n in range(NCHUNK):
                        last = nc.vector.max_index(top_at[:, n, :], top[:, n, :], gate[:, n, :])
                    link(last)
                    link(nc.vector.tensor_copy(top_e[:, :, :], top_at[:, :, 0:2]))
                if i == 6:
                    vec.wait_ge(e2x_done, 1)
                    link(nc.vector.tensor_scalar(row1[:, :], row2[:, :], 1.0, None, ALU.add))
                    link(nc.vector.reciprocal(tp[:, 0, :], row1[:, :]))
                    link(nc.vector.tensor_tensor(tp[:, 1, :], tp[:, 0, :], row2[:, :], ALU.mult))
                    link(nc.vector.tensor_tensor(wtok[:, :, :], iota_e[:, :, :], bc(top_e[:, :, 0]), ALU.is_equal))
                    link(nc.vector.tensor_tensor(wtok[:, :, :], wtok[:, :, :], bc(tp[:, 0, :]), ALU.mult))
                    link(nc.vector.tensor_tensor(wtmp[:, :, :], iota_e[:, :, :], bc(top_e[:, :, 1]), ALU.is_equal))
                    link(nc.vector.tensor_tensor(wtmp[:, :, :], wtmp[:, :, :], bc(tp[:, 1, :]), ALU.mult))
                    nc.vector.tensor_tensor(wtok[:, :, :], wtok[:, :, :], wtmp[:, :, :], ALU.add).then_inc(w_done, 1)

            vec.wait_ge(consts_done, 6)
            over_groups(vec, step, after, between)

            vec.wait_ge(b_in, 48)
            vec.wait_ge(w_done, 1)
            with vec.Fori(0, NU) as u:
                part = bass.ds(u * UNIT, UNIT)
                for e in range(NX):
                    vec.wait_ge(o_ready, u * NX + (e + 1))
                    src = bank[4 + e % 3]
                    if e == 0:
                        nc.vector.tensor_tensor(acc[:, part, :], src[:, :].rearrange("p (n c) -> p n c", c=C),
                                                bs2_b[:, :].unsqueeze(1).to_broadcast([P, UNIT, C]),
                                                ALU.add).then_inc(o_done, 1)
                    else:
                        vec.wait_ge(o_done, u * NX + e)
                        for c in range(UNIT):
                            at = bass.ds(u * UNIT + c, 1)
                            last = nc.vector.scalar_tensor_tensor(acc[:, at, :], src[:, c * P:(c + 1) * P],
                                                                  wtok[:, at, e - 1], acc[:, at, :], ALU.mult, ALU.add)
                        last.then_inc(o_done, 1)
                vec.wait_ge(g_done, u + 1)
                nc.vector.tensor_tensor(s_sum[:, part, :], s_sum[:, part, :], acc[:, part, :], ALU.mult).then_inc(m_done, 1)
                vec.wait_ge(m_done, u + 1)
                nc.vector.tensor_tensor(x_sb[:, part, :], x_sb[:, part, :], s_sum[:, part, :], ALU.add).then_inc(res_done, 1)


NAMES = ['L0_attn_x', 'L0_attn_Wq', 'L0_attn_Wk', 'L0_attn_Wv', 'L0_attn_Wo', 'L0_attn_W_feat',
         'L0_ffn_Wr1', 'L0_ffn_br1', 'L0_ffn_Wr2', 'L0_ffn_br2', 'L0_ffn_Ws1', 'L0_ffn_bs1', 'L0_ffn_Ws2',
         'L0_ffn_bs2', 'L0_ffn_We1', 'L0_ffn_be1', 'L0_ffn_We2', 'L0_ffn_be2']


def kernel(**inputs):
    import numpy as np
    import concourse.bacc as bacc
    from concourse.bass_utils import run_bass_kernel_spmd

    nc = bacc.Bacc("TRN2", target_bir_lowering=False, num_devices=1)
    arrays, args = {}, []
    for name in NAMES:
        a = np.ascontiguousarray(inputs[name])
        arrays[name] = a
        args.append(nc.dram_tensor(name, a.shape, mybir.dt.from_np(a.dtype), kind="ExternalInput").ap())
    shape = arrays['L0_attn_x'].shape
    out = nc.dram_tensor("out", shape, F32, kind="ExternalOutput").ap()
    build(nc, *args, out)
    return run_bass_kernel_spmd(nc, [arrays], core_ids=[0]).results[0]["out"]
```

```python
from contextlib import ExitStack

import concourse.bass as bass
import concourse.mybir as mybir

F32 = mybir.dt.float32
F32R = mybir.dt.float32r
U32 = mybir.dt.uint32
I32 = mybir.dt.int32
ALU = mybir.AluOpType
ACT = mybir.ActivationFunctionType
AX = mybir.AxisListType

P = 128
HD = 64
NF = 128
HG = 4
NCHUNK = 16
UNIT = 4
TU = UNIT * P
EV = HD + 1
LN_EPS = 1e-5
EPS = 1e-6


def build(nc, x, Wq, Wk, Wv, Wo, W_feat, Wr1, br1, Wr2, br2, Ws1, bs1, Ws2, bs2, We1, be1, We2, be2, out):
    T, C = x.shape[1], x.shape[2]
    H = Wq.shape[1] // HD
    NG = H // HG
    GW = HG * HD
    NU = NCHUNK // UNIT
    R = Wr1.shape[1]
    E, _, I = We1.shape
    IB = I // P
    TOP = 2
    TILES = TOP * NCHUNK + E - 1
    SHIFT = P.bit_length() - 1
    RING = 3
    assert TILES % RING == 0 and T == NCHUNK * P and C == P and W_feat.shape == (HD, NF)

    x_d = x.rearrange("a (n p) c -> p (a n) c", p=P)
    out_d = out.rearrange("a (n p) c -> p (a n) c", p=P)

    x_slots = nc.dram_tensor("x_slots", (TILES * P, C), F32, kind="Internal").ap()
    y_slots = nc.dram_tensor("y_slots", (TILES * P, C), F32, kind="Internal").ap()

    with ExitStack() as ctx:
        def sb(name, shape, dt=F32):
            return ctx.enter_context(nc.sbuf_tensor(name, shape, dt))

        def sem(name):
            return ctx.enter_context(nc.semaphore(name))

        x_sb = sb("x_sb", [P, NCHUNK, C])
        xn = sb("xn", [P, NCHUNK, C])
        xT_hi = sb("xT_hi", [P, T], F32R)
        xT_lo = sb("xT_lo", [P, T], F32R)
        ident = sb("ident", [P, P])
        stats = sb("stats", [P, NCHUNK, 6])
        mean_var = sb("mean_var", [P, NCHUNK, 2])
        rstd = sb("rstd", [P, NCHUNK])
        minus_half = sb("minus_half", [P, NCHUNK])
        minus_mean = sb("minus_mean", [P, NCHUNK])
        w_raw = sb("w_raw", [P, 3, GW])
        w_hi = sb("w_hi", [P, 3, GW], F32R)
        w_lo = sb("w_lo", [P, 3, GW], F32R)
        wo = sb("wo", [P, H * HD // P, C])
        wf_q = sb("wf_q", [P, 2, NF])
        area = sb("area", [P, 5 * HG * TU])
        phi = area[:, 0:4 * HG * TU].rearrange("p (u a h t) -> p u a h t", u=2, a=2, h=HG)
        stack = area[:, 4 * HG * TU:].rearrange("p (s h t) -> p s h t", s=2, h=2)
        hr = area[0:R + 1, 2 * HG * TU:2 * HG * TU + T]
        y_tiles = area[:, 0:TILES * C].rearrange("p (n c) -> p n c", c=C)
        x_tiles = area[:, TILES * C:2 * TILES * C].rearrange("p (n c) -> p n c", c=C)
        hid = area[:, 0:2 * I * UNIT].rearrange("p (s b t) -> p s b t", s=2, b=IB)
        v1 = sb("v1", [P, 2, UNIT, HG, EV])
        causal = sb("causal", [P, P])
        den = sb("den", [P, HG])
        places, used = {}, 0
        for name, size in (("probs", HG * P), ("k_tok", HG * NF), ("state", 2 * HG * EV), ("y", HG * HD), ("yT", 2 * P)):
            places[name] = slice(used, used + size)
            used += size
        small = sb("small", [P, used])
        probs = small[:, places["probs"]].rearrange("p (h q) -> p h q", h=HG)
        k_tok = small[:, places["k_tok"]].rearrange("p (h f) -> p h f", h=HG)
        state = small[:, places["state"]].rearrange("p (s h e) -> p s h e", s=2, h=HG)
        y = small[:, places["y"]].rearrange("p (h d) -> p h d", h=HG)
        yT = small[:, places["yT"]].rearrange("p (b t) -> p b t", b=2)
        h_tile = small[:, 0:RING * I].rearrange("p (s i) -> p s i", s=RING)
        hT_tile = small[:, RING * I:(RING + 1) * I].rearrange("p (b t) -> p b t", b=IB)
        s_sum = sb("s_sum", [P, NCHUNK, C])
        wr1 = sb("wr1", [P, P])
        xg_hi = sb("xg_hi", [P, RING, P], F32R)
        xg_lo = sb("xg_lo", [P, RING, P], F32R)
        wr1_hi, wr1_lo = xg_hi[:, 0, :], xg_lo[:, 0, :]
        br1_c = sb("br1_c", [R, 1])
        wr2 = sb("wr2", [R + 1, E])
        gate = sb("gate", [P, NCHUNK, E])
        row1 = sb("row1", [P, NCHUNK])
        row2 = sb("row2", [P, NCHUNK])
        top = sb("top", [P, NCHUNK, 8])
        top_at = sb("top_at", [P, NCHUNK, 8], U32)
        top_e = sb("top_e", [P, NCHUNK, 2])
        tp = sb("tp", [P, 2, NCHUNK])
        iota_e = sb("iota_e", [P, NCHUNK, E])
        wtok = sb("wtok", [P, NCHUNK, E])
        chosen = sb("chosen", [P, TOP, NCHUNK, E])
        wtmp = sb("wtmp", [P, NCHUNK, E])
        before = sb("before", [P, P])
        ones = sb("ones", [P, P])
        ranks = sb("ranks", [P, 2, NCHUNK, E])
        upto = sb("upto", [P, NCHUNK, E])
        count_i = sb("count_i", [P, E], I32)
        tiles_of = sb("tiles_of", [P, E])
        tile_end = sb("tile_end", [P, E])
        slot_base = sb("slot_base", [P, E])
        slot_f = sb("slot_f", [P, TOP, NCHUNK])
        slot = sb("slot", [P, TOP, NCHUNK], U32)
        iota_t = sb("iota_t", [P, TILES, E - 1])
        expert_f = sb("expert_f", [P, TILES])
        expert = sb("expert", [P, TILES], I32)
        wtokT = sb("wtokT", [P, P])
        be2_bd = sb("be2_bd", [P, NCHUNK, C])
        bs2_b = sb("bs2_b", [P, C])
        e1_raw = sb("e1_raw", [P, 2, I])
        e1_hi = sb("e1_hi", [P, E + 1, I], F32R)
        e1_lo = sb("e1_lo", [P, E + 1, I], F32R)
        s1_rows = sb("s1_rows", [P, P])
        s1_b = sb("s1_b", [P, IB])
        e1_b = sb("e1_b", [P, E, I])
        e2 = sb("e2", [P, E + 1, IB, C])
        acc = xn
        x_ring = e1_raw[:, 0, 0:RING * C].rearrange("p (s c) -> p s c", c=C)
        got = e1_raw[:, :, :].rearrange("p a (b k c) -> p (a b) k c", b=2, k=TOP)

        bank = [ctx.enter_context(nc.psum_tensor(f"bank{i}", [P, 512], F32)) for i in range(8)]
        PROJ, VY, FEAT, SCORE, KTOK, OUT, STATE = bank[0], bank[1], bank[2:4], bank[4], bank[5], bank[6], bank[7]

        x_in = [sem(f"x_in{i}") for i in range(NU)]
        w_in = [sem("wq_in"), sem("wk_in"), sem("wv_in")]
        wo_in, wf_in = sem("wo_in"), sem("wf_in")
        r_in, b_in, e2_in, bd_in = sem("r_in"), sem("b_in"), sem("e2_in"), sem("bd_in")
        e1_in = [sem("e1_in0"), sem("e1_in1")]
        out_done = sem("out_done")
        consts_done = sem("consts_done")
        bd_zero = sem("bd_zero")
        half_done = sem("half_done")
        var_done, eps_done, pow_done, rstd_done = sem("var_done"), sem("eps_done"), sem("pow_done"), sem("rstd_done")
        r_split = sem("r_split")
        w_hi_done = [sem("wq_hi_done"), sem("wk_hi_done"), sem("wv_hi_done")]
        w_split = [sem("wq_split"), sem("wk_split"), sem("wv_split")]
        hi_done = sem("hi_done")
        e1_split = sem("e1_split")
        xn_done, xn_half_done = sem("xn_done"), sem("xn_half_done")
        xt_ready, xhi_done, xlo_done = sem("xt_ready"), sem("xhi_done"), sem("xlo_done")
        dve = sem("dve")
        rh_ready, rh_done, lg_ready = sem("rh_ready"), sem("rh_done"), sem("lg_ready")
        lg_done, ex_done, d_done, e2x_done = sem("lg_done"), sem("ex_done"), sem("d_done"), sem("e2x_done")
        w_done, wt_ready, wt_done = sem("w_done"), sem("wt_ready"), sem("wt_done")
        proj_ready, q_copied, q_squared = sem("proj_ready"), sem("q_copied"), sem("q_squared")
        feat_ready, phi_done = sem("feat_ready"), sem("phi_done")
        score_ready, masked = sem("score_ready"), sem("masked")
        ktok_ready, ktok_done = sem("ktok_ready"), sem("ktok_done")
        outp_ready, y_done = sem("outp_ready"), sem("y_done")
        vy_ready, v_done, yt_ready, yt_done = sem("vy_ready"), sem("v_done"), sem("yt_ready"), sem("yt_done")
        den_done, lgs_done = sem("den_done"), sem("lgs_done")
        st_ready, st_done, s_added = sem("st_ready"), sem("st_done"), sem("s_added")
        chosen_done, rank_ready, rank_done, slots_done = sem("chosen_done"), sem("rank_ready"), sem("rank_done"), sem("slots_done")
        experts_done, scattered, zeroed = sem("experts_done"), sem("scattered"), sem("zeroed")
        xg_in = [sem(f"xg_in{i}") for i in range(RING)]
        h_ready, h_done = sem("h_ready"), sem("h_done")
        o_ready, o_done = sem("o_ready"), sem("o_done")
        t_placed, t_ready, t_hi, t_lo = sem("t_placed"), sem("t_ready"), sem("t_hi"), sem("t_lo")
        l1_ready, l1_biased, l1_done = sem("l1_ready"), sem("l1_biased"), sem("l1_done")
        ht_ready, ht_done = sem("ht_ready"), sem("ht_done")
        l2_ready, l2_done = sem("l2_ready"), sem("l2_done")
        stored, gathered, combined = sem("stored"), [sem(f"gathered{i}") for i in range(4)], sem("combined")
        g_done, m_done, res_done = sem("g_done"), sem("m_done"), sem("res_done")

        block = ctx.enter_context(nc.Block())

        FEAT_AHEAD, PROJ_AHEAD = 4, 5

        def group_0(step, after, between):
            for i in range(-PROJ_AHEAD, NCHUNK):
                step(0, i, NCHUNK)
                between(i)
            after(0)

        def other_groups(eng, step, after, between, first_chunk):
            end = NG * NCHUNK
            for i in range(-PROJ_AHEAD, 0):
                step(1, i, end)
            first_chunk()
            with eng.Fori(1, NG - 1) as g:
                for i in range(NCHUNK):
                    step(g, i, end)
                after(g)
            for i in range(NCHUNK):
                step(NG - 1, i, end)
                between(i)
            after(NG - 1)

        def proj_bank(i):
            return SCORE if i < 0 and (i + PROJ_AHEAD) % 2 else PROJ

        def ahead(g, i, by, end):
            return i + by >= 0 and not (isinstance(g, int) and g * NCHUNK + i + by >= end)

        def nothing(i):
            pass

        L1_AHEAD, X_AHEAD, PLACE_AHEAD = 2, 3, 4

        def over_tiles(eng, turn):
            for s in range(-PLACE_AHEAD, 0):
                turn(s, s % RING)
            last = TILES - PLACE_AHEAD // RING * RING - RING
            with eng.Fori(0, last // RING) as r:
                for k in range(RING):
                    turn(r * RING + k, k)
            for s in range(last, TILES):
                turn(s, s % RING)

        def within(s, by):
            return not isinstance(s, int) or 0 <= s + by < TILES

        RESPLIT = {9: (0, 14), 11: (1, 16), 12: (2, 16)}

        GATE_STEP = 12
        ZERO_DMAS = -(-TILES // NCHUNK)

        @block.sync
        def _(sp):
            for u in range(NU):
                sp.dma_start(x_sb[:, u * UNIT:(u + 1) * UNIT, :], x_d[:, u * UNIT:(u + 1) * UNIT, :]).then_inc(x_in[u], 16)
            for j, (src, arrived) in enumerate(((Wq, w_in[0]), (Wk, w_in[1]), (Wv, w_in[2]))):
                sp.dma_start(w_raw[:, j, :], src[:, 0:GW]).then_inc(arrived, 16)
            sp.wait_ge(bd_zero, 1)
            sp.dma_start(wr1[:, 0:R], Wr1).then_inc(r_in, 16)
            sp.dma_start(br1_c[:, :], br1.rearrange("(r a) -> r a", a=1)).then_inc(r_in, 16)
            sp.dma_start(wr2[0:R, :], Wr2).then_inc(r_in, 16)
            sp.dma_start(wr2[R:R + 1, :], br2.rearrange("(a e) -> a e", a=1)).then_inc(r_in, 16)
            sp.dma_start(wf_q[0:HD, 0, :], W_feat).then_inc(wf_in, 16)
            sp.dma_start(wf_q[HD:P, 1, :], W_feat).then_inc(wf_in, 16)
            sp.dma_start(wo[:, :, :], Wo.rearrange("(b p) c -> p b c", p=P)).then_inc(wo_in, 16)
            for j, src in enumerate((Wq, Wk, Wv)):
                sp.wait_ge(w_split[j], 1)
                sp.dma_start(w_raw[:, j, :], src[:, GW:2 * GW]).then_inc(w_in[j], 16)
            sp.wait_ge(bd_zero, 2)
            slots_by_row = x_slots.rearrange("(p n) c -> p n c", p=P)
            for n in range(0, TILES, NCHUNK):
                w = min(NCHUNK, TILES - n)
                sp.dma_start(slots_by_row[:, n:n + w, :], be2_bd[:, 0:w, :]).then_inc(zeroed, 16)
            for e in range(E + 1):
                if e >= 2:
                    sp.wait_ge(e1_split, e - 1)
                sp.dma_start(e1_raw[:, e % 2, :], Ws1 if e == E else We1[e]).then_inc(e1_in[e % 2], 16)
            sp.dma_start(s1_rows[0:IB, :], bs1.rearrange("(b p) -> b p", p=P)).then_inc(b_in, 16)
            sp.dma_start(bs2_b[:, :], bs2.rearrange("(a c) -> a c", a=1).broadcast_to([P, C])).then_inc(b_in, 16)
            sp.dma_start(e1_b[:, :, :], be1.rearrange("(a e) i -> a e i", a=1).broadcast_to([P, E, I])).then_inc(b_in, 16)
            sp.dma_start(e2[:, 0:E, :, :], We2.rearrange("e (b p) c -> p e b c", p=P)).then_inc(e2_in, 16)
            sp.dma_start(e2[:, E, :, :], Ws2.rearrange("(b p) c -> p b c", p=P)).then_inc(e2_in, 16)
            sp.wait_ge(zeroed, 16 * ZERO_DMAS)
            for n in range(NCHUNK):
                sp.dma_start(be2_bd[n * E:(n + 1) * E, n, :], be2).then_inc(bd_in, 16)
            sp.wait_ge(scattered, 16 * TOP * NCHUNK)
            sp.wait_ge(s_added, NCHUNK)
            per = TILES // RING
            for m in range(RING):
                sp.dma_start(x_tiles[:, m * per:(m + 1) * per, :],
                             x_slots[m * per * P:(m + 1) * per * P, :].rearrange("(n p) c -> p n c", p=P)).then_inc(xg_in[m], 16)
            with sp.Fori(1, NG - 1) as g:
                for j, src in enumerate((Wq, Wk, Wv)):
                    sp.wait_ge(w_split[j], g + 1)
                    sp.dma_start(w_raw[:, j, :], src[:, bass.ds((g + 1) * GW, GW)]).then_inc(w_in[j], 16)
            for u in range(NU):
                sp.wait_ge(res_done, u + 1)
                sp.dma_start(out_d[:, u * UNIT:(u + 1) * UNIT, :], x_sb[:, u * UNIT:(u + 1) * UNIT, :]).then_inc(out_done, 16)
            sp.wait_ge(out_done, 16 * NU)

        @block.gpsimd
        def _(pool):
            nc.gpsimd.memset(ident[:, :], 0.0).then_inc(consts_done, 1)
            pool.wait_ge(consts_done, 1)
            nc.gpsimd.affine_select(out=ident[:, :], in_=ident[:, :], compare_op=ALU.not_equal, fill=1.0, base=0,
                                    pattern=[[-1, P]], channel_multiplier=1).then_inc(consts_done, 1)
            nc.gpsimd.memset(minus_half[:, :], -0.5)
            nc.gpsimd.memset(s1_rows[:, :], 0.0)
            nc.gpsimd.memset(wr1[:, :], 0.0).then_inc(bd_zero, 1)
            nc.gpsimd.memset(ones[:, :], 1.0)
            nc.gpsimd.memset(before[:, :], 1.0)
            nc.gpsimd.iota(iota_t[:, :, :], pattern=[[1, TILES], [0, E - 1]], base=0, channel_multiplier=0,
                           allow_small_or_imprecise_dtypes=True)
            nc.gpsimd.iota(iota_e[:, :, :], pattern=[[0, NCHUNK], [1, E]], base=0, channel_multiplier=0,
                           allow_small_or_imprecise_dtypes=True)
            nc.gpsimd.memset(causal[:, :], 1.0).then_inc(consts_done, 1)
            pool.wait_ge(consts_done, 3)
            nc.gpsimd.affine_select(out=causal[:, :], in_=causal[:, :], compare_op=ALU.is_ge, fill=0.0, base=0,
                                    pattern=[[1, P]], channel_multiplier=-1)
            for u in range(NU):
                part = slice(u * UNIT, (u + 1) * UNIT)
                pool.wait_ge(var_done, u + 1)
                nc.gpsimd.tensor_scalar(rstd[:, part], mean_var[:, part, 1], LN_EPS, None, ALU.add).then_inc(eps_done, 1)
                pool.wait_ge(eps_done, u + 1)
                nc.gpsimd.tensor_tensor(rstd[:, part], rstd[:, part], minus_half[:, part], ALU.pow).then_inc(pow_done, 1)
            nc.gpsimd.affine_select(out=before[:, :], in_=before[:, :], compare_op=ALU.is_gt, fill=0.0, base=0,
                                    pattern=[[1, P]], channel_multiplier=-1).then_inc(consts_done, 1)
            splits = [0]

            def split(hi, lo, raw):
                nc.gpsimd.tensor_copy(hi, raw).then_inc(hi_done, 1)
                splits[0] += 1
                pool.wait_ge(hi_done, splits[0])
                return nc.gpsimd.tensor_tensor(lo, raw, hi.bitcast(F32), ALU.subtract)

            pool.wait_ge(r_in, 64)
            split(wr1_hi, wr1_lo, wr1[:, :]).then_inc(r_split, 1)
            nc.gpsimd.memset(v1[:, :, :, :, :], 1.0).then_inc(consts_done, 1)
            nc.gpsimd.memset(s_sum[:, :, :], 0.0).then_inc(consts_done, 1)
            nc.gpsimd.memset(be2_bd[:, :, :], 0.0).then_inc(bd_zero, 1)
            for e in range(E + 1):
                pool.wait_ge(e1_in[e % 2], 16 * (e // 2 + 1))
                split(e1_hi[:, e, :], e1_lo[:, e, :], e1_raw[:, e % 2, :]).then_inc(e1_split, 1)
            pool.wait_ge(slots_done, 1)
            pool.wait_ge(zeroed, 16 * ZERO_DMAS)
            for n in range(NCHUNK):
                for k in range(TOP):
                    nc.gpsimd.indirect_dma_start(x_slots, bass.IndirectOffsetOnAxis(ap=slot[:, k, n:n + 1], axis=0),
                                                 xn[:, n, :], None).then_inc(scattered, 16)
            by_tile = y_slots.rearrange("(n p) c -> p n c", p=P)
            with pool.Fori(0, TILES // RING) as r:
                pool.wait_ge(l2_done, r * RING + RING)
                at = bass.ds(r * RING, RING)
                nc.gpsimd.dma_start(by_tile[:, at, :], y_tiles[:, at, :]).then_inc(stored, 16)
            pool.wait_ge(stored, 16 * (TILES // RING))
            for n in range(NCHUNK):
                if n >= 4:
                    pool.wait_ge(combined, n - 3)
                for k in range(TOP):
                    nc.gpsimd.indirect_dma_start(got[:, n % 4, k, :], None, y_slots,
                                                 bass.IndirectOffsetOnAxis(ap=slot[:, k, n:n + 1], axis=0)).then_inc(gathered[n % 4], 16)

        @block.tensor
        def _(pe):
            def mm3(dst, l_hi, l_lo, r_hi, r_lo, start=True, stop=True):
                nc.tensor.matmul(dst, l_hi, r_hi, start=start, stop=False)
                nc.tensor.matmul(dst, l_hi, r_lo, start=False, stop=False)
                return nc.tensor.matmul(dst, l_lo, r_hi, start=False, stop=stop)

            pe.wait_ge(consts_done, 2)
            for u in range(NU):
                pe.wait_ge(xn_done, u + 1)
                pe.wait_ge(xn_half_done, u + 1)
                for c in range(UNIT):
                    last = nc.tensor.transpose(bank[u][:, c * P:(c + 1) * P], xn[:, u * UNIT + c, :], ident[:, :])
                last.then_inc(xt_ready, 1)

            router_bank = [bank[5], bank[6], bank[7], bank[5]]

            def step(g, i, end):
                n = g * NCHUNK + i
                u, c = (i // UNIT) % 2, i % UNIT
                attends = i >= 0
                if attends:
                    if c == 0:
                        pe.wait_ge(phi_done, n * 2 + 2 * UNIT)
                    for h in range(HG):
                        last = nc.tensor.matmul(SCORE[:, h * P:(h + 1) * P], phi[:, u, 1, h, c * P:(c + 1) * P],
                                                phi[:, u, 0, h, c * P:(c + 1) * P], start=True, stop=True)
                    last.then_inc(score_ready, 1)
                    if i < NCHUNK - 1:
                        for h in range(HG):
                            last = nc.tensor.transpose(KTOK[:, h * P:(h + 1) * P],
                                                       phi[:, u, 1, h, c * P:(c + 1) * P], ident[:, :])
                        last.then_inc(ktok_ready, 1)

                def feature(h):
                    j = n + FEAT_AHEAD
                    s = (i + FEAT_AHEAD) % 2
                    if h == 0:
                        pe.wait_ge(q_squared, j + 1)
                    if not isinstance(j, int) or j > 0:
                        pe.wait_ge(phi_done, j * 2 + (h - 1))
                    nc.tensor.matmul(FEAT[h][:, :], wf_q[:, h, :], stack[:, s, h, :],
                                     start=True, stop=True).then_inc(feat_ready, 1)

                def project():
                    b = (i + PROJ_AHEAD) % UNIT
                    t0 = (i + PROJ_AHEAD) % NCHUNK // UNIT * TU
                    if b == 0 and t0 == 0:
                        pe.wait_ge(w_split[0], g + (i + PROJ_AHEAD) // NCHUNK + 1)
                    if b == 2 and t0 == 0:
                        pe.wait_ge(w_split[1], g + (i + PROJ_AHEAD) // NCHUNK + 1)
                    if i >= 0:
                        pe.wait_ge(q_copied, n + PROJ_AHEAD)
                    elif i >= 2 - PROJ_AHEAD:
                        pe.wait_ge(q_copied, n + PROJ_AHEAD - 1)
                    cols = slice(b % 2 * P, b % 2 * P + P)
                    mm3(proj_bank(i)[:, :], w_hi[:, b // 2, cols], w_lo[:, b // 2, cols], xT_hi[:, t0:t0 + TU],
                        xT_lo[:, t0:t0 + TU]).then_inc(proj_ready, 1)

                if i < 0:
                    if g == 0 and i == -PROJ_AHEAD:
                        pe.wait_ge(xlo_done, 1)
                    if g == 0 and i == -PROJ_AHEAD + 1:
                        pe.wait_ge(xlo_done, NU)
                    project()

                if ahead(g, i, FEAT_AHEAD, end):
                    if i == -FEAT_AHEAD:
                        pe.wait_ge(wf_in, 32)
                    feature(0)

                if attends and i > 0:
                    pe.wait_ge(st_done, g * (NCHUNK - 1) + i)
                    for h in range(HG):
                        nc.tensor.matmul(OUT[:, h * EV:(h + 1) * EV], phi[:, u, 0, h, c * P:(c + 1) * P],
                                         state[:, i % 2, h, :], start=(h == 0), stop=False, skip_group_check=True)

                if i >= 0 and ahead(g, i, PROJ_AHEAD, end):
                    project()

                if attends:
                    pe.wait_ge(masked, n + 1)
                    if c == 0:
                        pe.wait_ge(v_done, n + UNIT)
                    for h in range(HG):
                        last = nc.tensor.matmul(OUT[:, h * EV:(h + 1) * EV], probs[:, h, :], v1[:, u, c, h, :],
                                                start=(i == 0 and h == 0), stop=True, skip_group_check=True)
                    last.then_inc(outp_ready, 1)

                if ahead(g, i, FEAT_AHEAD, end):
                    feature(1)

                if attends and i < NCHUNK - 1:
                    pe.wait_ge(ktok_done, g * (NCHUNK - 1) + (i + 1))
                    for h in range(HG):
                        last = nc.tensor.matmul(STATE[:, h * EV:(h + 1) * EV], k_tok[:, h, :], v1[:, u, c, h, :],
                                                start=True, stop=True)
                    if i == 0:
                        last.then_inc(st_ready, 1)
                if attends and i > 0:
                    output(g, i - 1, STATE)

                if ahead(g, i, FEAT_AHEAD, end):
                    j = (i + FEAT_AHEAD) % NCHUNK
                    if j == 0:
                        pe.wait_ge(w_split[2], g + (i + FEAT_AHEAD) // NCHUNK + 1)
                    if i > -FEAT_AHEAD:
                        pe.wait_ge(v_done, n + FEAT_AHEAD)
                    last = mm3(VY[:, 0:GW], xT_hi[:, j * P:(j + 1) * P], xT_lo[:, j * P:(j + 1) * P],
                               w_hi[:, 2, :], w_lo[:, 2, :])
                    last.then_inc(vy_ready, 1)
                if attends:
                    pe.wait_ge(y_done, n + 1)
                    for p in range(2):
                        last = nc.tensor.transpose(VY[:, GW + p * P:GW + (p + 1) * P], y[:, 2 * p:2 * p + 2, :],
                                                   ident[:, :])
                    last.then_inc(yt_ready, 1)

            def output(g, i, dst):
                pe.wait_ge(yt_done, g * NCHUNK + (i + 1))
                for p in range(2):
                    last = nc.tensor.matmul(dst[:, 384:384 + C], yT[:, p, :], wo[:, bass.ds(g * 2 + p, 1), :],
                                            start=(p == 0), stop=(p == 1))
                last.then_inc(st_ready, 1)

            def after(g):
                output(g, NCHUNK - 1, OUT)

            def between(i):
                u = i + PROJ_AHEAD
                if u < NU:
                    if u == 0:
                        pe.wait_ge(r_split, 1)
                    if u == NU - 1:
                        pe.wait_ge(rh_done, 1)
                    pe.wait_ge(xlo_done, u + 1)
                    mm3(router_bank[u][:, :], wr1_hi, wr1_lo, xT_hi[:, u * TU:(u + 1) * TU],
                        xT_lo[:, u * TU:(u + 1) * TU]).then_inc(rh_ready, 1)
                if u == NU:
                    pe.wait_ge(half_done, 1)
                    pe.wait_ge(rh_done, NU)
                    for n in range(NCHUNK):
                        last = nc.tensor.matmul(STATE[:, n * E:(n + 1) * E],
                                                hr[:, n * P:(n + 1) * P], wr2[:, :], start=True, stop=True)
                    last.then_inc(lg_ready, 1)
                    pe.wait_ge(lg_done, 1)
                if i == 9:
                    pe.wait_ge(chosen_done, 1)
                    nc.tensor.matmul(KTOK[:, 0:P], before[:, :], wtmp[:, :, :], start=True, stop=True)
                    nc.tensor.matmul(KTOK[:, P:2 * P], ones[:, :], wtmp[:, :, :], start=True,
                                     stop=True).then_inc(rank_ready, 1)
                    pe.wait_ge(rank_done, 1)

            pe.wait_ge(wo_in, 16)
            group_0(step, after, between)
            pe.wait_ge(s_added, NCHUNK)

            pe.wait_ge(w_done, 1)
            pe.wait_ge(b_in, 48)
            nc.tensor.transpose(bank[0][:, 0:P], wtok[:, :, :], ident[:, :])
            nc.tensor.transpose(bank[0][:, P:2 * P], s1_rows[:, :], ident[:, :]).then_inc(wt_ready, 1)
            pe.wait_ge(wt_done, 1)
            pe.wait_ge(e1_split, E + 1)
            pe.wait_ge(e2_in, 32)
            pe.wait_ge(bd_in, 16 * NCHUNK)

            def shared_first(u):
                for b in range(IB):
                    if u > 0:
                        pe.wait_ge(h_done, (u - 1) * IB + b + 1)
                    cols = slice(b * P, (b + 1) * P)
                    t = slice(u * TU, (u + 1) * TU)
                    mm3(bank[b][:, :], e1_hi[:, E, cols], e1_lo[:, E, cols], xT_hi[:, t], xT_lo[:, t]).then_inc(h_ready, 1)

            shared_first(0)
            for u in range(NU):
                if u + 1 < NU:
                    shared_first(u + 1)
                pe.wait_ge(h_done, (u + 1) * IB)
                if u >= 2:
                    pe.wait_ge(o_done, u - 1)
                dst = bank[4 + u % 2]
                nc.tensor.matmul(dst[:, :], wtokT[:, :], be2_bd[:, u * UNIT:(u + 1) * UNIT, :], start=True,
                                 stop=False, skip_group_check=True)
                for c in range(UNIT):
                    for b in range(IB):
                        last = nc.tensor.matmul(dst[:, c * P:(c + 1) * P], hid[:, u % 2, b, c * P:(c + 1) * P],
                                                e2[:, E, b, :], start=False, stop=(b == IB - 1), skip_group_check=True)
                last.then_inc(o_ready, 1)
            pe.wait_ge(o_done, NU)

            pe.wait_ge(experts_done, 1)

            experts = [pe.alloc_register(f"pe_expert{k}") for k in range(RING)]

            def expert_of(k):
                return pe.snap(experts[k], min_val=0, max_val=E - 1)

            def turn(s, k):
                if within(s, 0):
                    pe.wait_ge(l1_done, s + 1)
                    for b in range(IB):
                        last = nc.tensor.transpose(bank[4][:, b * P:(b + 1) * P], h_tile[:, k, b * P:(b + 1) * P], ident[:, :])
                    last.then_inc(ht_ready, 1)
                if within(s, X_AHEAD):
                    if not isinstance(s, int) or s > -X_AHEAD:
                        pe.wait_ge(t_lo, s + X_AHEAD)
                    pe.wait_ge(t_placed, s + (X_AHEAD + 1))
                    nc.tensor.transpose(bank[3][:, 0:P], x_ring[:, k, :], ident[:, :]).then_inc(t_ready, 1)
                if within(s, L1_AHEAD):
                    kk = (k + L1_AHEAD) % RING
                    if not within(s, X_AHEAD):
                        pe.wait_ge(t_lo, s + (L1_AHEAD + 1))
                    of = expert_of(kk)
                    mm3(bank[kk][:, :], xg_hi[:, kk, :], xg_lo[:, kk, :], e1_hi[:, bass.ds(of, 1), :],
                        e1_lo[:, bass.ds(of, 1), :]).then_inc(l1_ready, 1)
                if within(s, 0):
                    of = expert_of(k)
                if within(s, X_AHEAD):
                    pe.reg_load(experts[k], expert[0:1, bass.ds(s + X_AHEAD, 1)])
                if within(s, 0):
                    pe.wait_ge(ht_done, s + 1)
                    for b in range(IB):
                        last = nc.tensor.matmul(bank[5 + k][:, 0:C], hT_tile[:, b, :], e2[:, bass.ds(of, 1), b, :],
                                                start=(b == 0), stop=(b == IB - 1))
                    last.then_inc(l2_ready, 1)

            over_tiles(pe, turn)
            pe.wait_ge(l1_done, TILES)
            other_groups(pe, step, after, nothing, lambda: pe.wait_ge(l2_done, TILES))

        @block.scalar
        def _(act):
            def normalise(u):
                act.wait_ge(rstd_done, u + 1)
                for n in range(u * UNIT + UNIT // 2, (u + 1) * UNIT):
                    last = nc.scalar.activation(xn[:, n, :], x_sb[:, n, :], ACT.Identity, bias=minus_mean[:, n:n + 1],
                                                scale=rstd[:, n:n + 1])
                last.then_inc(xn_half_done, 1)

            def high_part(u):
                act.wait_ge(xt_ready, u + 1)
                nc.scalar.copy(xT_hi[:, u * TU:(u + 1) * TU], bank[u][:, :]).then_inc(xhi_done, 1)

            normalise(0)
            normalise(1)
            high_part(0)
            normalise(2)
            act.wait_ge(w_in[0], 16)
            nc.scalar.copy(w_hi[:, 0, :], w_raw[:, 0, :]).then_inc(w_hi_done[0], 1)
            high_part(1)
            normalise(3)
            high_part(2)
            high_part(3)
            for j in range(1, 3):
                act.wait_ge(w_in[j], 16)
                nc.scalar.copy(w_hi[:, j, :], w_raw[:, j, :]).then_inc(w_hi_done[j], 1)
            act.wait_ge(r_in, 64)
            router_bank = [bank[5], bank[6], bank[7], bank[5]]

            def step(g, i, end):
                n = g * NCHUNK + i
                if i in RESPLIT and not isinstance(g, int):
                    j, slots = RESPLIT[i]
                    act.wait_ge(w_in[j], g * 16 + 32)
                    act.wait_ge(vy_ready if j == 2 else proj_ready, g * NCHUNK + slots)
                    nc.scalar.copy(w_hi[:, j, :], w_raw[:, j, :]).then_inc(w_hi_done[j], 1)
                if 0 <= i < NCHUNK - 1:
                    act.wait_ge(ktok_ready, g * (NCHUNK - 1) + (i + 1))
                    nc.scalar.copy(k_tok[:, :, :], KTOK[:, :]).then_inc(ktok_done, 1)

                def features(h):
                    b, u = i % UNIT, (i + FEAT_AHEAD) // UNIT % 2
                    act.wait_ge(feat_ready, n * 2 + (2 * FEAT_AHEAD + h + 1))
                    nc.scalar.activation(phi[:, u, b // 2, b % 2 * 2 + h, :], FEAT[h][:, :], ACT.Exp).then_inc(phi_done, 1)

                if i >= 0 and ahead(g, i, FEAT_AHEAD, end):
                    features(0)
                if ahead(g, i, PROJ_AHEAD, end):
                    s = (i + PROJ_AHEAD) % 2
                    act.wait_ge(q_copied, n + PROJ_AHEAD + 1)
                    nc.scalar.activation(stack[HD:P, s, 0, :], stack[0:HD, s, 0, :], ACT.Square)
                    nc.scalar.activation(stack[0:HD, s, 1, :], stack[HD:P, s, 1, :], ACT.Square).then_inc(q_squared, 1)
                if i < 0 and ahead(g, i, FEAT_AHEAD, end):
                    features(0)
                if ahead(g, i, FEAT_AHEAD, end):
                    features(1)
                    act.wait_ge(vy_ready, n + FEAT_AHEAD + 1)
                    if i >= 0:
                        act.wait_ge(yt_ready, n + 1)
                    if i == -FEAT_AHEAD:
                        act.wait_ge(consts_done, 5)
                    nc.scalar.copy(v1[:, (i + FEAT_AHEAD) // UNIT % 2, i % UNIT, :, 0:HD],
                                   VY[:, 0:GW].rearrange("p (h d) -> p h d", d=HD)).then_inc(v_done, 1)
                if i >= 0:
                    act.wait_ge(yt_ready, n + 1)
                    nc.scalar.copy(yT[:, :, :], VY[:, GW:2 * GW]).then_inc(yt_done, 1)

            def after(g):
                pass

            def between(i):
                u = i + PROJ_AHEAD
                if u < NU:
                    act.wait_ge(rh_ready, u + 1)
                    nc.scalar.activation(hr[0:R, u * TU:(u + 1) * TU], router_bank[u][0:R, :], ACT.Relu,
                                         bias=br1_c[:, :]).then_inc(rh_done, 1)
                if i == 2:
                    act.wait_ge(lgs_done, 1)
                    nc.scalar.activation(gate[:, :, :], gate[:, :, :], ACT.Exp).then_inc(ex_done, 1)
                if i == 5:
                    act.wait_ge(d_done, 1)
                    nc.scalar.activation(row2[:, :], row2[:, :], ACT.Exp, scale=0.5).then_inc(e2x_done, 1)

            group_0(step, after, between)
            act.wait_ge(proj_ready, NCHUNK)
            act.wait_ge(vy_ready, NCHUNK)
            for j in range(3):
                act.wait_ge(w_in[j], 32)
                nc.scalar.copy(w_hi[:, j, :], w_raw[:, j, :]).then_inc(w_hi_done[j], 1)

            act.wait_ge(wt_ready, 1)
            nc.scalar.copy(wtokT[:, :], bank[0][:, 0:P])
            nc.scalar.copy(s1_b[:, :], bank[0][:, P:P + IB]).then_inc(wt_done, 1)
            act.wait_ge(wt_done, 1)
            for u in range(NU):
                for b in range(IB):
                    act.wait_ge(h_ready, u * IB + b + 1)
                    nc.scalar.activation(hid[:, u % 2, b, :], bank[b][:, :], ACT.Silu,
                                         bias=s1_b[:, b:b + 1]).then_inc(h_done, 1)

            def turn(s, k):
                if within(s, 0):
                    act.wait_ge(ht_ready, s + 1)
                    nc.scalar.copy(hT_tile[:, :, :], bank[4][:, :]).then_inc(ht_done, 1)
                if within(s, X_AHEAD):
                    act.wait_ge(t_ready, s + (X_AHEAD + 1))
                    nc.scalar.copy(xg_hi[:, k, :], bank[3][:, 0:P]).then_inc(t_hi, 1)
                if within(s, L1_AHEAD):
                    kk = (k + L1_AHEAD) % RING
                    act.wait_ge(l1_biased, s + (L1_AHEAD + 1))
                    nc.scalar.activation(h_tile[:, kk, :], h_tile[:, kk, :], ACT.Silu).then_inc(l1_done, 1)

            over_tiles(act, turn)
            act.wait_ge(stored, 16 * (TILES // RING))

            def gate_steps(i):
                if i == GATE_STEP:
                    act.wait_ge(combined, NCHUNK)
                    nc.scalar.activation(acc[:, :, :], acc[:, :, :], ACT.Silu).then_inc(g_done, 1)

            other_groups(act, step, after, gate_steps, lambda: None)

        @block.vector
        def _(vec):
            chain = [0]

            def link(ins):
                chain[0] += 1
                ins.then_inc(dve, 1)
                vec.wait_ge(dve, chain[0])

            nc.vector.memset(wf_q[HD:P, 0, :], -0.5)
            nc.vector.memset(wf_q[0:HD, 1, :], -0.5)
            nc.vector.memset(hr[R:R + 1, :], 1.0).then_inc(half_done, 1)
            def moments(u):
                vec.wait_ge(x_in[u], 16)
                for n in range(u * UNIT, (u + 1) * UNIT):
                    last = nc.vector.bn_stats(stats[:, n, :], x_sb[:, n, :])
                link(last)
                for n in range(u * UNIT, (u + 1) * UNIT):
                    last = nc.vector.bn_aggr(mean_var[:, n, :], stats[:, n, :])
                last.then_inc(var_done, 1)

            def scale(u):
                part = slice(u * UNIT, (u + 1) * UNIT)
                vec.wait_ge(pow_done, u + 1)
                nc.vector.scalar_tensor_tensor(minus_mean[:, part], mean_var[:, part, 0], -1.0, rstd[:, part],
                                               ALU.mult, ALU.mult).then_inc(rstd_done, 1)
                for n in range(u * UNIT, u * UNIT + UNIT // 2):
                    last = nc.vector.tensor_scalar(xn[:, n, :], x_sb[:, n, :], mean_var[:, n, 0:1], rstd[:, n:n + 1],
                                                   ALU.subtract, ALU.mult)
                last.then_inc(xn_done, 1)

            def low_part(u):
                vec.wait_ge(xhi_done, u + 1)
                t = slice(u * TU, (u + 1) * TU)
                nc.vector.tensor_tensor(xT_lo[:, t], bank[u][:, :], xT_hi[:, t].bitcast(F32),
                                        ALU.subtract).then_inc(xlo_done, 1)

            moments(0)
            moments(1)
            scale(0)
            moments(2)
            scale(1)
            moments(3)
            low_part(0)
            scale(2)
            scale(3)
            vec.wait_ge(w_hi_done[0], 1)
            nc.vector.tensor_tensor(w_lo[:, 0, :], w_raw[:, 0, :], w_hi[:, 0, :].bitcast(F32),
                                    ALU.subtract).then_inc(w_split[0], 1)
            for u in range(1, NU):
                low_part(u)
            for j in range(1, 3):
                vec.wait_ge(w_hi_done[j], 1)
                nc.vector.tensor_tensor(w_lo[:, j, :], w_raw[:, j, :], w_hi[:, j, :].bitcast(F32),
                                        ALU.subtract).then_inc(w_split[j], 1)

            def step(g, i, end):
                n = g * NCHUNK + i
                if i in RESPLIT and not isinstance(g, int):
                    j = RESPLIT[i][0]
                    vec.wait_ge(w_hi_done[j], g + 2)
                    nc.vector.tensor_tensor(w_lo[:, j, :], w_raw[:, j, :], w_hi[:, j, :].bitcast(F32),
                                            ALU.subtract).then_inc(w_split[j], 1)
                if i >= 0:
                    vec.wait_ge(score_ready, n + 1)
                    nc.vector.tensor_tensor(probs[:, :, :], SCORE[:, :].rearrange("p (h q) -> p h q", q=P),
                                            causal[:, :].unsqueeze(1).to_broadcast([P, HG, P]), ALU.mult).then_inc(masked, 1)
                if ahead(g, i, PROJ_AHEAD, end):
                    s = (i + PROJ_AHEAD) % 2
                    vec.wait_ge(proj_ready, n + PROJ_AHEAD + 1)
                    nc.vector.tensor_copy(stack[0:HD, s, 0, :], proj_bank(i)[0:HD, :])
                    nc.vector.tensor_copy(stack[HD:P, s, 1, :], proj_bank(i)[HD:P, :]).then_inc(q_copied, 1)
                if i >= 0:
                    vec.wait_ge(outp_ready, n + 1)
                    o = OUT[:, 0:HG * EV].rearrange("p (h e) -> p h e", e=EV)
                    nc.vector.tensor_scalar(den[:, :], o[:, :, HD], NF * EPS, None, ALU.add).then_inc(den_done, 1)
                    vec.wait_ge(den_done, n * 2 + 1)
                    nc.vector.reciprocal(den[:, :], den[:, :]).then_inc(den_done, 1)
                    vec.wait_ge(den_done, n * 2 + 2)
                    nc.vector.tensor_tensor(y[:, :, :], o[:, :, 0:HD], den[:, :].unsqueeze(2).to_broadcast([P, HG, HD]),
                                            ALU.mult).then_inc(y_done, 1)
                    vec.wait_ge(st_ready, g * (NCHUNK + 1) + (i + 1))
                    if i > 0:
                        gather(i - 1, STATE)
                    if i < NCHUNK - 1:
                        new, old = state[:, (i + 1) % 2, :, :], state[:, i % 2, :, :]
                        delta = STATE[:, 0:HG * EV].rearrange("p (h e) -> p h e", e=EV)
                        if i == 0:
                            nc.vector.tensor_copy(new, delta).then_inc(st_done, 1)
                        else:
                            vec.wait_ge(st_done, g * (NCHUNK - 1) + i)
                            nc.vector.tensor_tensor(new, delta, old, ALU.add).then_inc(st_done, 1)

            def gather(i, src):
                nc.vector.tensor_tensor(s_sum[:, i, :], src[:, 384:384 + C], s_sum[:, i, :], ALU.add).then_inc(s_added, 1)

            def after(g):
                vec.wait_ge(st_ready, g * (NCHUNK + 1) + (NCHUNK + 1))
                gather(NCHUNK - 1, OUT)

            def bc(a, k=E):
                return a.unsqueeze(2).to_broadcast([P, NCHUNK, k])

            def between(i):
                if i == -1:
                    vec.wait_ge(lg_ready, 1)
                    nc.vector.tensor_copy(gate[:, :, :], STATE[:, 0:NCHUNK * E]).then_inc(lg_done, 1)
                if i == 1:
                    vec.wait_ge(lg_done, 1)
                    link(nc.vector.tensor_reduce(row1[:, :], gate[:, :, :], AX.X, ALU.max))
                    nc.vector.tensor_tensor(gate[:, :, :], gate[:, :, :], bc(row1[:, :]), ALU.subtract).then_inc(lgs_done, 1)
                if i == 3:
                    vec.wait_ge(ex_done, 1)
                    link(nc.vector.tensor_reduce(row1[:, :], gate[:, :, :], AX.X, ALU.add))
                    link(nc.vector.reciprocal(row1[:, :], row1[:, :]))
                    link(nc.vector.tensor_tensor(gate[:, :, :], gate[:, :, :], bc(row1[:, :]), ALU.mult))
                    for n in range(NCHUNK):
                        last = nc.vector.max(top[:, n, :], gate[:, n, :])
                    link(last)
                    nc.vector.tensor_tensor(row2[:, :], top[:, :, 1], top[:, :, 0], ALU.subtract).then_inc(d_done, 1)
                if i == 4:
                    for n in range(NCHUNK):
                        last = nc.vector.max_index(top_at[:, n, :], top[:, n, :], gate[:, n, :])
                    link(last)
                    link(nc.vector.tensor_copy(top_e[:, :, :], top_at[:, :, 0:2]))
                if i == 6:
                    vec.wait_ge(e2x_done, 1)
                    link(nc.vector.tensor_scalar(row1[:, :], row2[:, :], 1.0, None, ALU.add))
                    link(nc.vector.reciprocal(tp[:, 0, :], row1[:, :]))
                    nc.vector.tensor_tensor(tp[:, 1, :], tp[:, 0, :], row2[:, :], ALU.mult)
                    for k in range(TOP):
                        last = nc.vector.tensor_tensor(chosen[:, k, :, :], iota_e[:, :, :], bc(top_e[:, :, k]), ALU.is_equal)
                    link(last)
                    nc.vector.tensor_tensor(wtmp[:, :, :], chosen[:, 0, :, :], chosen[:, 1, :, :], ALU.add).then_inc(chosen_done, 1)
                if i == 9:
                    vec.wait_ge(rank_ready, 1)
                    nc.vector.tensor_copy(ranks[:, :, :, :], KTOK[:, 0:2 * P]).then_inc(rank_done, 1)
                    vec.wait_ge(rank_done, 1)
                    for e in range(E):
                        last = nc.vector.tensor_tensor_scan(upto[:, :, e], ones[:, 0:NCHUNK], ranks[:, 1, :, e], 0.0,
                                                            ALU.mult, ALU.add)
                    link(last)
                    link(nc.vector.tensor_scalar(count_i[:, :], upto[:, NCHUNK - 1, :], float(P - 1), None, ALU.add))
                    link(nc.vector.tensor_scalar(count_i[:, :], count_i[:, :], SHIFT, None, ALU.arith_shift_right))
                    link(nc.vector.tensor_copy(tiles_of[:, :], count_i[:, :]))
                    link(nc.vector.tensor_tensor_scan(tile_end[:, :], ones[:, 0:E], tiles_of[:, :], 0.0, ALU.mult, ALU.add))
                    link(nc.vector.tensor_tensor(slot_base[:, :], tile_end[:, :], tiles_of[:, :], ALU.subtract))
                    link(nc.vector.tensor_scalar(slot_base[:, :], slot_base[:, :], float(P), None, ALU.mult))
                    link(nc.vector.tensor_tensor(upto[:, :, :], upto[:, :, :], ranks[:, 1, :, :], ALU.subtract))
                    link(nc.vector.tensor_tensor(upto[:, :, :], upto[:, :, :], ranks[:, 0, :, :], ALU.add))
                    link(nc.vector.tensor_tensor(upto[:, :, :], upto[:, :, :],
                                                 slot_base[:, :].unsqueeze(1).to_broadcast([P, NCHUNK, E]), ALU.add))
                    for k in range(TOP):
                        link(nc.vector.tensor_tensor(wtmp[:, :, :], upto[:, :, :], chosen[:, k, :, :], ALU.mult))
                        link(nc.vector.tensor_reduce(slot_f[:, k, :], wtmp[:, :, :], AX.X, ALU.add))
                    nc.vector.tensor_copy(slot[:, :, :], slot_f[:, :, :]).then_inc(slots_done, 1)
                if i == 10:
                    link(nc.vector.tensor_tensor(iota_t[:, :, :], iota_t[:, :, :],
                                                 tile_end[:, 0:E - 1].unsqueeze(1).to_broadcast([P, TILES, E - 1]), ALU.is_ge))
                    link(nc.vector.tensor_reduce(expert_f[:, :], iota_t[:, :, :], AX.X, ALU.add))
                    nc.vector.tensor_copy(expert[:, :], expert_f[:, :]).then_inc(experts_done, 1)
                    for k in range(TOP):
                        last = nc.vector.tensor_tensor(chosen[:, k, :, :], chosen[:, k, :, :], bc(tp[:, k, :]), ALU.mult)
                    link(last)
                    nc.vector.tensor_tensor(wtok[:, :, :], chosen[:, 0, :, :], chosen[:, 1, :, :], ALU.add).then_inc(w_done, 1)

            vec.wait_ge(consts_done, 6)
            group_0(step, after, between)
            for j in range(3):
                vec.wait_ge(w_hi_done[j], 2)
                nc.vector.tensor_tensor(w_lo[:, j, :], w_raw[:, j, :], w_hi[:, j, :].bitcast(F32),
                                        ALU.subtract).then_inc(w_split[j], 1)

            vec.wait_ge(b_in, 48)
            vec.wait_ge(scattered, 16 * TOP * NCHUNK)
            for u in range(NU):
                vec.wait_ge(o_ready, u + 1)
                nc.vector.tensor_tensor(acc[:, u * UNIT:(u + 1) * UNIT, :],
                                        bank[4 + u % 2][:, :].rearrange("p (n c) -> p n c", c=C),
                                        bs2_b[:, :].unsqueeze(1).to_broadcast([P, UNIT, C]), ALU.add).then_inc(o_done, 1)
            vec.wait_ge(experts_done, 1)
            for m in range(RING):
                vec.wait_ge(xg_in[m], 16)

            def turn(s, k):
                if within(s, L1_AHEAD):
                    kk = (k + L1_AHEAD) % RING
                    of = nc.vector.value_load(expert[0:1, bass.ds(s + L1_AHEAD, 1)], min_val=0, max_val=E - 1)
                    vec.wait_ge(l1_ready, s + (L1_AHEAD + 1))
                    nc.vector.tensor_tensor(h_tile[:, kk, :], bank[kk][:, :], e1_b[:, bass.ds(of, 1), :], ALU.add).then_inc(l1_biased, 1)
                if within(s, X_AHEAD):
                    vec.wait_ge(t_hi, s + (X_AHEAD + 1))
                    nc.vector.tensor_tensor(xg_lo[:, k, :], bank[3][:, 0:P], xg_hi[:, k, :].bitcast(F32),
                                            ALU.subtract).then_inc(t_lo, 1)
                if within(s, PLACE_AHEAD):
                    nc.vector.tensor_copy(x_ring[:, (k + PLACE_AHEAD) % RING, :],
                                          x_tiles[:, bass.ds(s + PLACE_AHEAD, 1), :]).then_inc(t_placed, 1)
                if within(s, 0):
                    vec.wait_ge(l2_ready, s + 1)
                    nc.vector.tensor_copy(y_tiles[:, bass.ds(s, 1), :], bank[5 + k][:, 0:C]).then_inc(l2_done, 1)

            over_tiles(vec, turn)

            def finish(u):
                part = slice(u * UNIT, (u + 1) * UNIT)
                nc.vector.tensor_tensor(s_sum[:, part, :], s_sum[:, part, :], acc[:, part, :], ALU.mult).then_inc(m_done, 1)
                vec.wait_ge(m_done, u + 1)
                nc.vector.tensor_tensor(x_sb[:, part, :], x_sb[:, part, :], s_sum[:, part, :], ALU.add).then_inc(res_done, 1)

            def combine(i):
                if 1 <= i < 9:
                    for n in (2 * i - 2, 2 * i - 1):
                        vec.wait_ge(gathered[n % 4], 16 * TOP * (n // 4 + 1))
                        link(nc.vector.scalar_tensor_tensor(acc[:, n, :], got[:, n % 4, 0, :], tp[:, 0, n:n + 1],
                                                            acc[:, n, :], ALU.mult, ALU.add))
                        nc.vector.scalar_tensor_tensor(acc[:, n, :], got[:, n % 4, 1, :], tp[:, 1, n:n + 1],
                                                       acc[:, n, :], ALU.mult, ALU.add).then_inc(combined, 1)
                if i > GATE_STEP:
                    if i == GATE_STEP + 1:
                        vec.wait_ge(g_done, 1)
                    finish(i - GATE_STEP - 1)

            other_groups(vec, step, after, combine, lambda: None)
            vec.wait_ge(s_added, NG * NCHUNK)
            finish(NU - 1)


NAMES = ['L0_attn_x', 'L0_attn_Wq', 'L0_attn_Wk', 'L0_attn_Wv', 'L0_attn_Wo', 'L0_attn_W_feat',
         'L0_ffn_Wr1', 'L0_ffn_br1', 'L0_ffn_Wr2', 'L0_ffn_br2', 'L0_ffn_Ws1', 'L0_ffn_bs1', 'L0_ffn_Ws2',
         'L0_ffn_bs2', 'L0_ffn_We1', 'L0_ffn_be1', 'L0_ffn_We2', 'L0_ffn_be2']


def kernel(**inputs):
    import numpy as np
    import concourse.bacc as bacc
    from concourse.bass_utils import run_bass_kernel_spmd

    nc = bacc.Bacc("TRN2", target_bir_lowering=False, num_devices=1)
    arrays, args = {}, []
    for name in NAMES:
        a = np.ascontiguousarray(inputs[name])
        arrays[name] = a
        args.append(nc.dram_tensor(name, a.shape, mybir.dt.from_np(a.dtype), kind="ExternalInput").ap())
    shape = arrays['L0_attn_x'].shape
    out = nc.dram_tensor("out", shape, F32, kind="ExternalOutput").ap()
    build(nc, *args, out)
    return run_bass_kernel_spmd(nc, [arrays], core_ids=[0]).results[0]["out"]
```

```python
from contextlib import ExitStack

import concourse.bass as bass
import concourse.mybir as mybir

F32 = mybir.dt.float32
F32R = mybir.dt.float32r
U32 = mybir.dt.uint32
I32 = mybir.dt.int32
ALU = mybir.AluOpType
ACT = mybir.ActivationFunctionType
AX = mybir.AxisListType

P = 128
HD = 64
NF = 128
HG = 4
NCHUNK = 16
UNIT = 4
TU = UNIT * P
EV = HD + 1
LN_EPS = 1e-5
EPS = 1e-6


def build(nc, x, Wq, Wk, Wv, Wo, W_feat, Wr1, br1, Wr2, br2, Ws1, bs1, Ws2, bs2, We1, be1, We2, be2, out):
    T, C = x.shape[1], x.shape[2]
    H = Wq.shape[1] // HD
    NG = H // HG
    GW = HG * HD
    NU = NCHUNK // UNIT
    R = Wr1.shape[1]
    E, _, I = We1.shape
    IB = I // P
    TOP = 2
    TILES = TOP * NCHUNK + E - 1
    SHIFT = P.bit_length() - 1
    RING = 3
    assert TILES % RING == 0 and T == NCHUNK * P and C == P and W_feat.shape == (HD, NF)

    x_d = x.rearrange("a (n p) c -> p (a n) c", p=P)
    out_d = out.rearrange("a (n p) c -> p (a n) c", p=P)

    x_slots = nc.dram_tensor("x_slots", (TILES * P, C), F32, kind="Internal").ap()
    y_slots = nc.dram_tensor("y_slots", (TILES * P, C), F32, kind="Internal").ap()

    with ExitStack() as ctx:
        def sb(name, shape, dt=F32):
            return ctx.enter_context(nc.sbuf_tensor(name, shape, dt))

        def sem(name):
            return ctx.enter_context(nc.semaphore(name))

        x_sb = sb("x_sb", [P, NCHUNK, C])
        xn = sb("xn", [P, NCHUNK, C])
        xT_hi = sb("xT_hi", [P, T], F32R)
        xT_lo = sb("xT_lo", [P, T], F32R)
        ident = sb("ident", [P, P])
        stats = sb("stats", [P, NCHUNK, 6])
        mean_var = sb("mean_var", [P, NCHUNK, 2])
        rstd = sb("rstd", [P, NCHUNK])
        minus_half = sb("minus_half", [P, NCHUNK])
        minus_mean = sb("minus_mean", [P, NCHUNK])
        w_raw = sb("w_raw", [P, 3, GW])
        w_hi = sb("w_hi", [P, 3, GW], F32R)
        w_lo = sb("w_lo", [P, 3, GW], F32R)
        wo = sb("wo", [P, H * HD // P, C])
        wf_hi = sb("wf_hi", [P, 2, NF], F32R)
        wf_lo = sb("wf_lo", [P, 2, NF], F32R)
        area = sb("area", [P, 4 * HG * TU])
        phi = area[:, 0:4 * HG * TU].rearrange("p (u a h t) -> p u a h t", u=2, a=2, h=HG)
        hr = area[0:R + 1, 2 * HG * TU:2 * HG * TU + T]
        hid = area[:, 2 * I * UNIT:].rearrange("p (s b t) -> p s b t", s=2, b=IB)
        v1 = sb("v1", [P, 2, UNIT, HG, EV])
        causal = sb("causal", [P, P])
        den = sb("den", [P, HG])
        places, used = {}, 0
        for name, size in (("probs", HG * P), ("k_tok", HG * NF), ("state", 2 * HG * EV), ("y", HG * HD), ("yT", 2 * P)):
            places[name] = slice(used, used + size)
            used += size
        small = sb("small", [P, used])
        probs = small[:, places["probs"]].rearrange("p (h q) -> p h q", h=HG)
        k_tok = small[:, places["k_tok"]].rearrange("p (h f) -> p h f", h=HG)
        state = small[:, places["state"]].rearrange("p (s h e) -> p s h e", s=2, h=HG)
        y = small[:, places["y"]].rearrange("p (h d) -> p h d", h=HG)
        yT = small[:, places["yT"]].rearrange("p (b t) -> p b t", b=2)
        h_tile = small[:, 0:RING * I].rearrange("p (s i) -> p s i", s=RING)
        hT_tile = small[:, RING * I:(RING + 1) * I].rearrange("p (b t) -> p b t", b=IB)
        s_sum = sb("s_sum", [P, NCHUNK, C])
        wr1 = small[:, 0:P]
        wf_raw = small[:, P:P + 2 * NF].rearrange("p (h f) -> p h f", h=2)
        xg_hi = sb("xg_hi", [P, RING, P], F32R)
        xg_lo = sb("xg_lo", [P, RING, P], F32R)
        wr1_hi, wr1_lo = xg_hi[:, 0, :], xg_lo[:, 0, :]
        br1_c = sb("br1_c", [R, 1])
        wr2 = sb("wr2", [R + 1, E])
        gate = sb("gate", [P, NCHUNK, E])
        row1 = sb("row1", [P, NCHUNK])
        row2 = sb("row2", [P, NCHUNK])
        top = sb("top", [P, NCHUNK, 8])
        top_at = sb("top_at", [P, NCHUNK, 8], U32)
        top_e = sb("top_e", [P, NCHUNK, 2])
        tp = sb("tp", [P, 2, NCHUNK])
        iota_e = sb("iota_e", [P, NCHUNK, E])
        wtok = sb("wtok", [P, NCHUNK, E])
        chosen = sb("chosen", [P, TOP, NCHUNK, E])
        wtmp = gate
        before = sb("before", [P, P])
        ones = sb("ones", [P, P])
        ranks = sb("ranks", [P, 2, NCHUNK, E])
        upto = sb("upto", [P, NCHUNK, E])
        count_i = sb("count_i", [P, E], I32)
        tiles_of = sb("tiles_of", [P, E])
        tile_end = sb("tile_end", [P, E])
        slot_base = sb("slot_base", [P, E])
        slot_f = sb("slot_f", [P, TOP, NCHUNK])
        slot = sb("slot", [P, TOP, NCHUNK], U32)
        iota_t = sb("iota_t", [P, TILES, E - 1])
        expert_f = sb("expert_f", [P, TILES])
        expert = sb("expert", [P, TILES], I32)
        wtokT = sb("wtokT", [P, P])
        be2_bd = sb("be2_bd", [P, NCHUNK, C])
        bs2_b = sb("bs2_b", [P, C])
        e1_raw = sb("e1_raw", [P, 2, I])
        e1_hi = sb("e1_hi", [P, E + 1, I], F32R)
        e1_lo = sb("e1_lo", [P, E + 1, I], F32R)
        EARLY = E + 1 - 4 * TU // I
        stack_hi = e1_hi[:, EARLY:, :].rearrange("p e i -> p (e i)").rearrange("p (s h t) -> p s h t", s=2, h=2)
        stack_lo = e1_lo[:, EARLY:, :].rearrange("p e i -> p (e i)").rearrange("p (s h t) -> p s h t", s=2, h=2)
        s1_rows = sb("s1_rows", [P, P])
        s1_b = sb("s1_b", [P, IB])
        e1_b = sb("e1_b", [P, E, I])
        squares = e1_b[:, 0:2, :]
        e2 = sb("e2", [P, E + 1, IB, C])
        acc = xn
        x_ring = sb("x_ring", [P, RING, C])
        y_ring = sb("y_ring", [P, RING, C])
        got = e1_raw[:, :, :].rearrange("p a (b k c) -> p (a b) k c", b=2, k=TOP)

        bank = [ctx.enter_context(nc.psum_tensor(f"bank{i}", [P, 512], F32)) for i in range(8)]
        PROJ, VY, FEAT, SCORE, KTOK, OUT, STATE = bank[0], bank[1], bank[2:4], bank[4], bank[5], bank[6], bank[7]

        x_in = [sem(f"x_in{i}") for i in range(NU)]
        w_in = [sem("wq_in"), sem("wk_in"), sem("wv_in")]
        wo_in, wf_in = sem("wo_in"), sem("wf_in")
        r_in, b_in, e2_in, bd_in, e1b_in = sem("r_in"), sem("b_in"), sem("e2_in"), sem("bd_in"), sem("e1b_in")
        e1_in = [sem("e1_in0"), sem("e1_in1")]
        out_done = sem("out_done")
        consts_done = sem("consts_done")
        bd_zero = sem("bd_zero")
        half_done = sem("half_done")
        var_done, eps_done, pow_done, rstd_done = sem("var_done"), sem("eps_done"), sem("pow_done"), sem("rstd_done")
        r_split = sem("r_split")
        w_hi_done = [sem("wq_hi_done"), sem("wk_hi_done"), sem("wv_hi_done")]
        w_split = [sem("wq_split"), sem("wk_split"), sem("wv_split")]
        hi_done = sem("hi_done")
        e1_split, late_split = sem("e1_split"), sem("late_split")
        xn_done, xn_half_done = sem("xn_done"), sem("xn_half_done")
        xt_ready, xhi_done, xlo_done = sem("xt_ready"), sem("xhi_done"), sem("xlo_done")
        dve = sem("dve")
        rh_ready, rh_done, lg_ready = sem("rh_ready"), sem("rh_done"), sem("lg_ready")
        lg_done, ex_done, d_done, e2x_done = sem("lg_done"), sem("ex_done"), sem("d_done"), sem("e2x_done")
        w_done, wt_ready, wt_done = sem("w_done"), sem("wt_ready"), sem("wt_done")
        wf_high, wf_split = sem("wf_high"), sem("wf_split")
        proj_ready = sem("proj_ready")
        q_high, q_low, squared, sq_high = sem("q_high"), sem("q_low"), sem("squared"), sem("sq_high")
        sq_low = [sem("sq0_low"), sem("sq1_low")]
        feat_ready, phi_done = sem("feat_ready"), sem("phi_done")
        score_ready, masked = sem("score_ready"), sem("masked")
        ktok_ready, ktok_done = sem("ktok_ready"), sem("ktok_done")
        outp_ready, y_done = sem("outp_ready"), sem("y_done")
        vy_ready, v_done, yt_ready, yt_done = sem("vy_ready"), sem("v_done"), sem("yt_ready"), sem("yt_done")
        den_done, lgs_done = sem("den_done"), sem("lgs_done")
        st_ready, st_done, s_added = sem("st_ready"), sem("st_done"), sem("s_added")
        chosen_done, rank_ready, rank_done, slots_done = sem("chosen_done"), sem("rank_ready"), sem("rank_done"), sem("slots_done")
        experts_done, zeroed = sem("experts_done"), sem("zeroed")
        scattered = [sem(f"scattered{u}") for u in range(NU)]
        tile_in = [sem(f"tile_in{i}") for i in range(RING)]
        h_ready, h_done = sem("h_ready"), sem("h_done")
        o_ready, o_done = sem("o_ready"), sem("o_done")
        t_ready, t_hi, t_lo = sem("t_ready"), sem("t_hi"), sem("t_lo")
        l1_ready, l1_biased, l1_done = sem("l1_ready"), sem("l1_biased"), sem("l1_done")
        ht_ready, ht_done = sem("ht_ready"), sem("ht_done")
        l2_ready, l2_done = sem("l2_ready"), sem("l2_done")
        stored = [sem(f"stored{i}") for i in range(RING)]
        gathered, combined = [sem(f"gathered{i}") for i in range(4)], sem("combined")
        g_done, m_done, res_done = sem("g_done"), sem("m_done"), sem("res_done")
        pool_m_done, pool_res_done = sem("pool_m_done"), sem("pool_res_done")

        block = ctx.enter_context(nc.Block())

        FEAT_AHEAD, PROJ_AHEAD = 4, 5
        KEPT = NCHUNK + FEAT_AHEAD

        def group_0(step, after, between):
            for i in range(-PROJ_AHEAD, NCHUNK):
                step(0, i, (0, KEPT))
                between(i)
            after(0)

        def slot_kept(step):
            step(1, -1, (KEPT, NG * NCHUNK))

        def other_groups(eng, step, after, between, first_chunk):
            slots = (KEPT, NG * NCHUNK)
            first_chunk()
            with eng.Fori(1, NG - 1) as g:
                for i in range(NCHUNK):
                    step(g, i, slots)
                after(g)
            for i in range(NCHUNK):
                step(NG - 1, i, slots)
                between(i)
            after(NG - 1)

        def proj_bank(i):
            return SCORE if i < 0 and (i + PROJ_AHEAD) % 2 else PROJ

        def ahead(g, i, by, slots):
            return not isinstance(g, int) or slots[0] <= g * NCHUNK + i + by < slots[1]

        HEADS = ((slice(0, HD), 0), (slice(HD, P), 1))

        def nothing(i):
            pass

        L1_AHEAD, X_AHEAD, LOAD_AHEAD = 2, RING, 2 * RING
        assert TILES > 2 * LOAD_AHEAD

        def over_tiles(eng, turn, shared_end, attention_start):
            for s in range(-LOAD_AHEAD, RING):
                turn(s, s % RING, s // RING)
                if s == -L1_AHEAD:
                    shared_end()
            with eng.Fori(1, (TILES - LOAD_AHEAD) // RING) as r:
                for k in range(RING):
                    turn(r * RING + k, k, r)
            for s in range(TILES - LOAD_AHEAD, TILES):
                turn(s, s % RING, s // RING)
                if s == TILES - 1 - L1_AHEAD:
                    attention_start()

        def within(s, by):
            return not isinstance(s, int) or 0 <= s + by < TILES

        RESPLIT = {9: (0, 14), 11: (1, 16), 12: (2, 16)}

        GATHERS = {i: (i // 3 * 4 + 2, i // 3 * 4 + 3) if i % 3 == 2 else (i // 3 * 4 + i % 3,) for i in range(NCHUNK // 4 * 3)}
        GATES = {12: (0,), 13: (1,), 14: (2, 3)}
        POOL_PARTS = tuple((u * UNIT, (u + 1) * UNIT) for u in range(NU - 1))
        DVE_PARTS = ((NCHUNK - UNIT, NCHUNK - 1), (NCHUNK - 1, NCHUNK))
        ROUTER = {-5: (0, 1), -4: (2, 3)}
        LOGITS = {-3: (0, 1), -2: (2,), -1: (3,)}
        RANK_STEP = 5
        WEIGHTS_STEP = NCHUNK - 2
        ZERO_DMAS = -(-TILES // NCHUNK)

        @block.sync
        def _(sp):
            for u in range(NU):
                sp.dma_start(x_sb[:, u * UNIT:(u + 1) * UNIT, :], x_d[:, u * UNIT:(u + 1) * UNIT, :]).then_inc(x_in[u], 16)
            for j, (src, arrived) in enumerate(((Wq, w_in[0]), (Wk, w_in[1]), (Wv, w_in[2]))):
                sp.dma_start(w_raw[:, j, :], src[:, 0:GW]).then_inc(arrived, 16)
            sp.wait_ge(bd_zero, 1)
            sp.dma_start(wr1[:, 0:R], Wr1).then_inc(r_in, 16)
            sp.dma_start(br1_c[:, :], br1.rearrange("(r a) -> r a", a=1)).then_inc(r_in, 16)
            sp.dma_start(wr2[0:R, :], Wr2).then_inc(r_in, 16)
            sp.dma_start(wr2[R:R + 1, :], br2.rearrange("(a e) -> a e", a=1)).then_inc(r_in, 16)
            sp.dma_start(wf_raw[0:HD, 0, :], W_feat).then_inc(wf_in, 16)
            sp.dma_start(wf_raw[HD:P, 1, :], W_feat).then_inc(wf_in, 16)
            sp.dma_start(wo[:, :, :], Wo.rearrange("(b p) c -> p b c", p=P)).then_inc(wo_in, 16)
            for j, src in enumerate((Wq, Wk, Wv)):
                sp.wait_ge(w_split[j], 1)
                sp.dma_start(w_raw[:, j, :], src[:, GW:2 * GW]).then_inc(w_in[j], 16)

            def first_layer(e):
                if e >= EARLY + 2:
                    sp.wait_ge(late_split, e - 1 - EARLY)
                elif e >= 2:
                    sp.wait_ge(e1_split, e - 1)
                sp.dma_start(e1_raw[:, e % 2, :], Ws1 if e == 0 else We1[e - 1]).then_inc(e1_in[e % 2], 16)

            first_layer(0)
            first_layer(1)
            sp.wait_ge(bd_zero, 2)
            slots_by_row = x_slots.rearrange("(p n) c -> p n c", p=P)
            for n in range(0, TILES, NCHUNK):
                w = min(NCHUNK, TILES - n)
                sp.dma_start(slots_by_row[:, n:n + w, :], be2_bd[:, 0:w, :]).then_inc(zeroed, 16)
            sp.dma_start(s1_rows[0:IB, :], bs1.rearrange("(b p) -> b p", p=P)).then_inc(b_in, 16)
            sp.dma_start(bs2_b[:, :], bs2.rearrange("(a c) -> a c", a=1).broadcast_to([P, C])).then_inc(b_in, 16)
            sp.dma_start(e2[:, 0:E, :, :], We2.rearrange("e (b p) c -> p e b c", p=P)).then_inc(e2_in, 16)
            sp.dma_start(e2[:, E, :, :], Ws2.rearrange("(b p) c -> p b c", p=P)).then_inc(e2_in, 16)
            for e in range(2, EARLY + 2):
                first_layer(e)
            sp.wait_ge(zeroed, 16 * ZERO_DMAS)
            for n in range(NCHUNK):
                sp.dma_start(be2_bd[n * E:(n + 1) * E, n, :], be2).then_inc(bd_in, 16)
            for h in range(2):
                sp.wait_ge(sq_low[h], KEPT)
            sp.wait_ge(feat_ready, 2 * KEPT)
            sp.dma_start(e1_b[:, :, :], be1.rearrange("(a e) i -> a e i", a=1).broadcast_to([P, E, I])).then_inc(e1b_in, 16)
            for e in range(EARLY + 2, E + 1):
                first_layer(e)
            for u in range(NU):
                sp.wait_ge(scattered[u], 16 * TOP * UNIT)
            x_by_tile = x_slots.rearrange("(n p) c -> p n c", p=P)
            y_by_tile = y_slots.rearrange("(n p) c -> p n c", p=P)

            def turn(s, k, r):
                if within(s, LOAD_AHEAD):
                    if not isinstance(s, int) or s >= -X_AHEAD:
                        sp.wait_ge(t_ready, s + (X_AHEAD + 1))
                    sp.dma_start(x_ring[:, k, :], x_by_tile[:, bass.ds(s + LOAD_AHEAD, 1), :]).then_inc(tile_in[k], 16)
                if within(s, 0):
                    sp.wait_ge(l2_done, s + 1)
                    sp.dma_start(y_by_tile[:, bass.ds(s, 1), :], y_ring[:, k, :]).then_inc(stored[k], 16)

            over_tiles(sp, turn, lambda: None, lambda: None)
            with sp.Fori(1, NG - 1) as g:
                for j, src in enumerate((Wq, Wk, Wv)):
                    sp.wait_ge(w_split[j], g + 1)
                    sp.dma_start(w_raw[:, j, :], src[:, bass.ds((g + 1) * GW, GW)]).then_inc(w_in[j], 16)
            for parts, complete in ((POOL_PARTS, pool_res_done), (DVE_PARTS, res_done)):
                for j, (first, upto) in enumerate(parts):
                    sp.wait_ge(complete, j + 1)
                    sp.dma_start(out_d[:, first:upto, :], x_sb[:, first:upto, :]).then_inc(out_done, 16)
            sp.wait_ge(out_done, 16 * (len(POOL_PARTS) + len(DVE_PARTS)))

        @block.gpsimd
        def _(pool):
            nc.gpsimd.memset(ident[:, :], 0.0).then_inc(consts_done, 1)
            pool.wait_ge(consts_done, 1)
            nc.gpsimd.affine_select(out=ident[:, :], in_=ident[:, :], compare_op=ALU.not_equal, fill=1.0, base=0,
                                    pattern=[[-1, P]], channel_multiplier=1).then_inc(consts_done, 1)
            nc.gpsimd.memset(minus_half[:, :], -0.5)
            nc.gpsimd.memset(s1_rows[:, :], 0.0)
            nc.gpsimd.memset(wr1[:, :], 0.0).then_inc(bd_zero, 1)
            nc.gpsimd.memset(ones[:, :], 1.0)
            nc.gpsimd.memset(before[:, :], 1.0)
            nc.gpsimd.iota(iota_t[:, :, :], pattern=[[1, TILES], [0, E - 1]], base=0, channel_multiplier=0,
                           allow_small_or_imprecise_dtypes=True)
            nc.gpsimd.iota(iota_e[:, :, :], pattern=[[0, NCHUNK], [1, E]], base=0, channel_multiplier=0,
                           allow_small_or_imprecise_dtypes=True)
            nc.gpsimd.memset(causal[:, :], 1.0).then_inc(consts_done, 1)
            pool.wait_ge(consts_done, 3)
            nc.gpsimd.affine_select(out=causal[:, :], in_=causal[:, :], compare_op=ALU.is_ge, fill=0.0, base=0,
                                    pattern=[[1, P]], channel_multiplier=-1)
            for u in range(NU):
                part = slice(u * UNIT, (u + 1) * UNIT)
                pool.wait_ge(var_done, u + 1)
                nc.gpsimd.tensor_scalar(rstd[:, part], mean_var[:, part, 1], LN_EPS, None, ALU.add).then_inc(eps_done, 1)
                pool.wait_ge(eps_done, u + 1)
                nc.gpsimd.tensor_tensor(rstd[:, part], rstd[:, part], minus_half[:, part], ALU.pow).then_inc(pow_done, 1)
            nc.gpsimd.affine_select(out=before[:, :], in_=before[:, :], compare_op=ALU.is_gt, fill=0.0, base=0,
                                    pattern=[[1, P]], channel_multiplier=-1).then_inc(consts_done, 1)
            splits = [0]

            def split(hi, lo, raw):
                nc.gpsimd.tensor_copy(hi, raw).then_inc(hi_done, 1)
                splits[0] += 1
                pool.wait_ge(hi_done, splits[0])
                return nc.gpsimd.tensor_tensor(lo, raw, hi.bitcast(F32), ALU.subtract)

            pool.wait_ge(r_in, 64)
            split(wr1_hi, wr1_lo, wr1[:, :]).then_inc(r_split, 1)
            nc.gpsimd.memset(v1[:, :, :, :, HD:EV], 1.0).then_inc(consts_done, 1)

            pool.wait_ge(r_split, 1)
            pool.wait_ge(consts_done, 5)

            def step(g, i, slots):
                if ahead(g, i, PROJ_AHEAD, slots):
                    s = (i + PROJ_AHEAD) % 2
                    slot_end = g * NCHUNK + (i + PROJ_AHEAD + 1)

                    def low(rows, h):
                        return nc.gpsimd.tensor_tensor(stack_lo[rows, s, h, :], squares[rows, s, :],
                                                       stack_hi[rows, s, h, :].bitcast(F32), ALU.subtract)

                    if not isinstance(slot_end, int) or slot_end > 1:
                        pool.wait_ge(sq_low[0], slot_end - 1)
                        pool.wait_ge(sq_low[1], slot_end - 1)
                    pool.wait_ge(sq_high, slot_end * 2 - 1)
                    low(slice(HD, P), 0).then_inc(sq_low[0], 1)
                    if i >= 0:
                        pool.wait_ge(sq_low[0], slot_end)
                        pool.wait_ge(sq_high, slot_end * 2)
                        low(slice(0, HD), 1).then_inc(sq_low[1], 1)

            def scatter(k, n):
                nc.gpsimd.indirect_dma_start(x_slots, bass.IndirectOffsetOnAxis(ap=slot[:, k, n:n + 1], axis=0),
                                             xn[:, n, :], None).then_inc(scattered[n // UNIT], 16)

            SCATTER_STEP = RANK_STEP + 3

            def first_layer(e):
                pool.wait_ge(e1_in[e % 2], 16 * (e // 2 + 1))
                split(e1_hi[:, e, :], e1_lo[:, e, :], e1_raw[:, e % 2, :]).then_inc(e1_split, 1)

            def between(i):
                if -1 <= i < EARLY + 1:
                    pool.wait_ge(sq_low[0], i + PROJ_AHEAD + 1)
                    pool.wait_ge(sq_low[1], i + PROJ_AHEAD + 1)
                if i == -1:
                    nc.gpsimd.memset(s_sum[:, :, :], 0.0).then_inc(consts_done, 1)
                    pool.wait_ge(consts_done, 6)
                if i == 0:
                    nc.gpsimd.memset(be2_bd[:, :, :], 0.0).then_inc(bd_zero, 1)
                    pool.wait_ge(bd_zero, 2)
                if 1 <= i < EARLY + 1:
                    first_layer(i - 1)
                    pool.wait_ge(e1_split, i)
                if i >= SCATTER_STEP:
                    if i == SCATTER_STEP:
                        pool.wait_ge(slots_done, 1)
                        pool.wait_ge(zeroed, 16 * ZERO_DMAS)
                    n = i - SCATTER_STEP
                    for m in range(n, NCHUNK if i == NCHUNK - 1 else n + 1):
                        for k in range(TOP):
                            scatter(k, m)
                    if i + 1 + PROJ_AHEAD < KEPT:
                        pool.wait_ge(scattered[n // UNIT], 16 * TOP * (n % UNIT + 1))

            def after(g):
                pass

            group_0(step, after, between)
            def gather_chunks(i):
                for n in GATHERS.get(i, ()):
                    if n == 0:
                        for k in range(RING):
                            pool.wait_ge(stored[k], 16 * (TILES // RING))
                    if n >= 4:
                        pool.wait_ge(combined, n - 3)
                    for k in range(TOP):
                        nc.gpsimd.indirect_dma_start(got[:, n % 4, k, :], None, y_slots,
                                                     bass.IndirectOffsetOnAxis(ap=slot[:, k, n:n + 1], axis=0)).then_inc(gathered[n % 4], 16)
                for n in GATHERS.get(i, ()):
                    pool.wait_ge(gathered[n % 4], 16 * TOP * (n // 4 + 1))

            slot_kept(step)
            other_groups(pool, step, after, gather_chunks, lambda: None)
            for j, (first, upto) in enumerate(POOL_PARTS):
                part = slice(first, upto)
                pool.wait_ge(g_done, j + 1)
                pool.wait_ge(s_added, (NG - 1) * NCHUNK + upto)
                nc.gpsimd.tensor_tensor(s_sum[:, part, :], s_sum[:, part, :], acc[:, part, :], ALU.mult).then_inc(pool_m_done, 1)
                pool.wait_ge(pool_m_done, j + 1)
                nc.gpsimd.tensor_tensor(x_sb[:, part, :], x_sb[:, part, :], s_sum[:, part, :], ALU.add).then_inc(pool_res_done, 1)

        @block.tensor
        def _(pe):
            def mm3(dst, l_hi, l_lo, r_hi, r_lo, start=True, stop=True):
                nc.tensor.matmul(dst, l_hi, r_hi, start=start, stop=False)
                nc.tensor.matmul(dst, l_hi, r_lo, start=False, stop=False)
                return nc.tensor.matmul(dst, l_lo, r_hi, start=False, stop=stop)

            pe.wait_ge(consts_done, 2)
            for u in range(NU):
                pe.wait_ge(xn_done, u + 1)
                pe.wait_ge(xn_half_done, u + 1)
                for c in range(UNIT):
                    last = nc.tensor.transpose(bank[u][:, c * P:(c + 1) * P], xn[:, u * UNIT + c, :], ident[:, :])
                last.then_inc(xt_ready, 1)

            router_bank = [bank[5], bank[6], bank[7], bank[5]]

            def step(g, i, slots):
                n = g * NCHUNK + i
                u, c = (i // UNIT) % 2, i % UNIT
                attends = i >= 0
                if attends:
                    if c == 0:
                        pe.wait_ge(phi_done, n * 2 + 2 * UNIT)
                    for h in range(HG):
                        last = nc.tensor.matmul(SCORE[:, h * P:(h + 1) * P], phi[:, u, 1, h, c * P:(c + 1) * P],
                                                phi[:, u, 0, h, c * P:(c + 1) * P], start=True, stop=True)
                    last.then_inc(score_ready, 1)
                    if i < NCHUNK - 1:
                        if isinstance(g, int) and g == 0 and i == RANK_STEP + 1:
                            pe.wait_ge(rank_done, 1)
                        for h in range(HG):
                            last = nc.tensor.transpose(KTOK[:, h * P:(h + 1) * P],
                                                       phi[:, u, 1, h, c * P:(c + 1) * P], ident[:, :])
                        last.then_inc(ktok_ready, 1)

                def feature(h):
                    j = n + FEAT_AHEAD
                    s = (i + FEAT_AHEAD) % 2
                    if h == 0:
                        pe.wait_ge(q_low, j + 1)
                    pe.wait_ge(sq_low[h], j + 1)
                    if not isinstance(j, int) or j > 0:
                        pe.wait_ge(phi_done, j * 2 + (h - 1))
                    mm3(FEAT[h][:, :], wf_hi[:, h, :], wf_lo[:, h, :], stack_hi[:, s, h, :],
                        stack_lo[:, s, h, :]).then_inc(feat_ready, 1)

                def project():
                    b = (i + PROJ_AHEAD) % UNIT
                    t0 = (i + PROJ_AHEAD) % NCHUNK // UNIT * TU
                    if b == 0 and t0 == 0:
                        pe.wait_ge(w_split[0], g + (i + PROJ_AHEAD) // NCHUNK + 1)
                    if b == 2 and t0 == 0:
                        pe.wait_ge(w_split[1], g + (i + PROJ_AHEAD) // NCHUNK + 1)
                    if i >= 2 - PROJ_AHEAD:
                        left = n + (PROJ_AHEAD if i >= 0 else PROJ_AHEAD - 1)
                        pe.wait_ge(q_low, left)
                    cols = slice(b % 2 * P, b % 2 * P + P)
                    mm3(proj_bank(i)[:, :], w_hi[:, b // 2, cols], w_lo[:, b // 2, cols], xT_hi[:, t0:t0 + TU],
                        xT_lo[:, t0:t0 + TU]).then_inc(proj_ready, 1)

                def values():
                    j = (i + FEAT_AHEAD) % NCHUNK
                    if j == 0:
                        pe.wait_ge(w_split[2], g + (i + FEAT_AHEAD) // NCHUNK + 1)
                    if i > -FEAT_AHEAD:
                        pe.wait_ge(v_done, n + FEAT_AHEAD)
                    last = mm3(VY[:, 0:GW], xT_hi[:, j * P:(j + 1) * P], xT_lo[:, j * P:(j + 1) * P],
                               w_hi[:, 2, :], w_lo[:, 2, :])
                    last.then_inc(vy_ready, 1)

                if i < 0:
                    if g == 0 and i == -PROJ_AHEAD:
                        pe.wait_ge(xlo_done, 1)
                    if g == 0 and i == -PROJ_AHEAD + 1:
                        pe.wait_ge(xlo_done, NU)
                    project()
                    if ahead(g, i, FEAT_AHEAD, slots):
                        values()
                elif ahead(g, i, PROJ_AHEAD, slots):
                    project()

                if ahead(g, i, FEAT_AHEAD, slots):
                    if i == -FEAT_AHEAD:
                        pe.wait_ge(wf_split, 1)
                    feature(0)

                if attends and i > 0:
                    pe.wait_ge(st_done, g * (NCHUNK - 1) + i)
                    for h in range(HG):
                        nc.tensor.matmul(OUT[:, h * EV:(h + 1) * EV], phi[:, u, 0, h, c * P:(c + 1) * P],
                                         state[:, i % 2, h, :], start=(h == 0), stop=False, skip_group_check=True)

                if attends:
                    pe.wait_ge(masked, n + 1)
                    if c == 0:
                        pe.wait_ge(v_done, n + UNIT)
                    for h in range(HG):
                        last = nc.tensor.matmul(OUT[:, h * EV:(h + 1) * EV], probs[:, h, :], v1[:, u, c, h, :],
                                                start=(i == 0 and h == 0), stop=True, skip_group_check=True)
                    last.then_inc(outp_ready, 1)

                if ahead(g, i, FEAT_AHEAD, slots):
                    feature(1)

                if attends and i < NCHUNK - 1:
                    pe.wait_ge(ktok_done, g * (NCHUNK - 1) + (i + 1))
                    for h in range(HG):
                        last = nc.tensor.matmul(STATE[:, h * EV:(h + 1) * EV], k_tok[:, h, :], v1[:, u, c, h, :],
                                                start=True, stop=True)
                    if i == 0:
                        last.then_inc(st_ready, 1)
                if attends and i > 0:
                    output(g, i - 1, STATE)

                if i >= 0 and ahead(g, i, FEAT_AHEAD, slots):
                    values()
                if attends:
                    pe.wait_ge(y_done, n + 1)
                    for p in range(2):
                        last = nc.tensor.transpose(VY[:, GW + p * P:GW + (p + 1) * P], y[:, 2 * p:2 * p + 2, :],
                                                   ident[:, :])
                    last.then_inc(yt_ready, 1)

            def output(g, i, dst):
                pe.wait_ge(yt_done, g * NCHUNK + (i + 1))
                for p in range(2):
                    last = nc.tensor.matmul(dst[:, 384:384 + C], yT[:, p, :], wo[:, bass.ds(g * 2 + p, 1), :],
                                            start=(p == 0), stop=(p == 1))
                last.then_inc(st_ready, 1)

            def after(g):
                if not isinstance(g, int) or g > 0:
                    output(g, NCHUNK - 1, OUT)

            def between(i):
                for u in ROUTER.get(i, ()):
                    if u == 0:
                        pe.wait_ge(r_split, 1)
                    if u == NU - 1:
                        pe.wait_ge(rh_done, 1)
                    pe.wait_ge(xlo_done, u + 1)
                    mm3(router_bank[u][:, :], wr1_hi, wr1_lo, xT_hi[:, u * TU:(u + 1) * TU],
                        xT_lo[:, u * TU:(u + 1) * TU]).then_inc(rh_ready, 1)
                for u in LOGITS.get(i, ()):
                    if u == 0:
                        pe.wait_ge(half_done, 1)
                        pe.wait_ge(rh_done, NU)
                    for m in range(u * UNIT, (u + 1) * UNIT):
                        last = nc.tensor.matmul(OUT[:, m * E:(m + 1) * E],
                                                hr[:, m * P:(m + 1) * P], wr2[:, :], start=True, stop=True)
                    if u == NU - 1:
                        last.then_inc(lg_ready, 1)
                if i == WEIGHTS_STEP:
                    pe.wait_ge(w_done, 1)
                    pe.wait_ge(b_in, 32)
                    pe.wait_ge(ktok_done, NCHUNK - 1)
                    nc.tensor.transpose(KTOK[:, 0:P], wtok[:, :, :], ident[:, :])
                    nc.tensor.transpose(KTOK[:, P:2 * P], s1_rows[:, :], ident[:, :]).then_inc(wt_ready, 1)
                if i == RANK_STEP:
                    pe.wait_ge(chosen_done, 1)
                    nc.tensor.matmul(KTOK[:, 0:P], before[:, :], wtmp[:, :, :], start=True, stop=True)
                    nc.tensor.matmul(KTOK[:, P:2 * P], ones[:, :], wtmp[:, :, :], start=True,
                                     stop=True).then_inc(rank_ready, 1)

            pe.wait_ge(wo_in, 16)
            group_0(step, after, between)
            def shared_first(u):
                for b in range(IB):
                    if u == 0 and b == 1:
                        output(0, NCHUNK - 1, OUT)
                    if u > 0:
                        pe.wait_ge(h_done, (u - 1) * IB + b + 1)
                    cols = slice(b * P, (b + 1) * P)
                    t = slice(u * TU, (u + 1) * TU)
                    mm3(bank[b][:, :], e1_hi[:, 0, cols], e1_lo[:, 0, cols], xT_hi[:, t], xT_lo[:, t]).then_inc(h_ready, 1)

            def shared_second(u):
                pe.wait_ge(h_done, (u + 1) * IB)
                if u >= 2:
                    pe.wait_ge(o_done, u - 1)
                dst = bank[4 + u % 2]
                nc.tensor.matmul(dst[:, :], wtokT[:, :], be2_bd[:, u * UNIT:(u + 1) * UNIT, :], start=True,
                                 stop=False, skip_group_check=True)
                for c in range(UNIT):
                    for b in range(IB):
                        last = nc.tensor.matmul(dst[:, c * P:(c + 1) * P], hid[:, u % 2, b, c * P:(c + 1) * P],
                                                e2[:, E, b, :], start=False, stop=(b == IB - 1), skip_group_check=True)
                last.then_inc(o_ready, 1)

            pe.wait_ge(e1_split, 1)
            pe.wait_ge(phi_done, 2 * KEPT)
            pe.wait_ge(v_done, KEPT)
            shared_first(0)
            shared_first(1)
            pe.wait_ge(e2_in, 32)
            pe.wait_ge(bd_in, 16 * NCHUNK)
            pe.wait_ge(wt_done, 1)
            for u in range(NU - 1):
                if u > 0:
                    shared_first(u + 1)
                shared_second(u)
            pe.wait_ge(h_done, NU * IB)
            pe.wait_ge(e1_split, EARLY)
            pe.wait_ge(late_split, E + 1 - EARLY)
            pe.wait_ge(experts_done, 1)

            experts = [pe.alloc_register(f"pe_expert{k}") for k in range(RING)]

            def expert_of(k):
                return pe.snap(experts[k], min_val=0, max_val=E - 1)

            def turn(s, k, r):
                if within(s, 0):
                    if isinstance(s, int) and s == 0:
                        pe.wait_ge(o_done, NU)
                    pe.wait_ge(l1_done, s + 1)
                    for b in range(IB):
                        last = nc.tensor.transpose(bank[4][:, b * P:(b + 1) * P], h_tile[:, k, b * P:(b + 1) * P], ident[:, :])
                    last.then_inc(ht_ready, 1)
                if within(s, X_AHEAD):
                    if not isinstance(s, int) or s > -X_AHEAD:
                        pe.wait_ge(t_lo, s + X_AHEAD)
                    pe.wait_ge(tile_in[k], (r + X_AHEAD // RING + 1) * 16)
                    nc.tensor.transpose(bank[3][:, 0:P], x_ring[:, k, :], ident[:, :]).then_inc(t_ready, 1)
                if within(s, L1_AHEAD):
                    kk = (k + L1_AHEAD) % RING
                    if not within(s, X_AHEAD):
                        pe.wait_ge(t_lo, s + (L1_AHEAD + 1))
                    of = expert_of(kk)
                    mm3(bank[kk][:, :], xg_hi[:, kk, :], xg_lo[:, kk, :], e1_hi[:, 1:, :][:, bass.ds(of, 1), :],
                        e1_lo[:, 1:, :][:, bass.ds(of, 1), :]).then_inc(l1_ready, 1)
                if within(s, 0):
                    of = expert_of(k)
                if within(s, X_AHEAD):
                    pe.reg_load(experts[k], expert[0:1, bass.ds(s + X_AHEAD, 1)])
                if within(s, 0):
                    for b in range(IB):
                        if b % (IB // 2) == 0:
                            pe.wait_ge(ht_done, s * 2 + (b // (IB // 2) + 1))
                        last = nc.tensor.matmul(bank[5 + k][:, 0:C], hT_tile[:, b, :], e2[:, bass.ds(of, 1), b, :],
                                                start=(b == 0), stop=(b == IB - 1))
                    last.then_inc(l2_ready, 1)

            over_tiles(pe, turn, lambda: shared_second(NU - 1), lambda: slot_kept(step))
            other_groups(pe, step, after, nothing, lambda: pe.wait_ge(l2_done, TILES))

        @block.scalar
        def _(act):
            def normalise(u):
                act.wait_ge(rstd_done, u + 1)
                for n in range(u * UNIT + UNIT // 2, (u + 1) * UNIT):
                    last = nc.scalar.activation(xn[:, n, :], x_sb[:, n, :], ACT.Identity, bias=minus_mean[:, n:n + 1],
                                                scale=rstd[:, n:n + 1])
                last.then_inc(xn_half_done, 1)

            def high_part(u):
                act.wait_ge(xt_ready, u + 1)
                nc.scalar.copy(xT_hi[:, u * TU:(u + 1) * TU], bank[u][:, :]).then_inc(xhi_done, 1)

            normalise(0)
            normalise(1)
            high_part(0)
            normalise(2)
            act.wait_ge(w_in[0], 16)
            nc.scalar.copy(w_hi[:, 0, :], w_raw[:, 0, :]).then_inc(w_hi_done[0], 1)
            high_part(1)
            normalise(3)
            high_part(2)
            high_part(3)
            for j in range(1, 3):
                act.wait_ge(w_in[j], 16)
                nc.scalar.copy(w_hi[:, j, :], w_raw[:, j, :]).then_inc(w_hi_done[j], 1)
            act.wait_ge(r_in, 64)
            router_bank = [bank[5], bank[6], bank[7], bank[5]]

            def step(g, i, slots):
                n = g * NCHUNK + i
                if i in RESPLIT and (not isinstance(g, int) or g == 0):
                    j, readers = RESPLIT[i]
                    act.wait_ge(w_in[j], g * 16 + 32)
                    act.wait_ge(vy_ready if j == 2 else proj_ready, g * NCHUNK + readers)
                    nc.scalar.copy(w_hi[:, j, :], w_raw[:, j, :]).then_inc(w_hi_done[j], 1)
                if 0 <= i < NCHUNK - 1:
                    act.wait_ge(ktok_ready, g * (NCHUNK - 1) + (i + 1))
                    nc.scalar.copy(k_tok[:, :, :], KTOK[:, :]).then_inc(ktok_done, 1)

                def features(h):
                    b, u = i % UNIT, (i + FEAT_AHEAD) // UNIT % 2
                    act.wait_ge(feat_ready, n * 2 + (2 * FEAT_AHEAD + h + 1))
                    nc.scalar.activation(phi[:, u, b // 2, b % 2 * 2 + h, :], FEAT[h][:, :], ACT.Exp).then_inc(phi_done, 1)

                def values():
                    act.wait_ge(vy_ready, n + FEAT_AHEAD + 1)
                    if i >= 0:
                        act.wait_ge(yt_ready, n + 1)
                    if i == -FEAT_AHEAD:
                        act.wait_ge(consts_done, 5)
                    nc.scalar.copy(v1[:, (i + FEAT_AHEAD) // UNIT % 2, i % UNIT, :, 0:HD],
                                   VY[:, 0:GW].rearrange("p (h d) -> p h d", d=HD)).then_inc(v_done, 1)

                if ahead(g, i, PROJ_AHEAD, slots):
                    s = (i + PROJ_AHEAD) % 2
                    act.wait_ge(proj_ready, n + PROJ_AHEAD + 1)
                    nc.scalar.activation(squares[HD:P, s, :], proj_bank(i)[0:HD, :], ACT.Square)
                    nc.scalar.activation(squares[0:HD, s, :], proj_bank(i)[HD:P, :], ACT.Square).then_inc(squared, 1)
                    act.wait_ge(squared, n + PROJ_AHEAD + 1)
                    nc.scalar.copy(stack_hi[HD:P, s, 0, :], squares[HD:P, s, :]).then_inc(sq_high, 1)
                    nc.scalar.copy(stack_hi[0:HD, s, 1, :], squares[0:HD, s, :]).then_inc(sq_high, 1)
                    if i >= 0:
                        for rows, h in HEADS:
                            last = nc.scalar.copy(stack_hi[rows, s, h, :], proj_bank(i)[rows, :])
                        last.then_inc(q_high, 1)
                if i < 0 and ahead(g, i, FEAT_AHEAD, slots):
                    values()
                if ahead(g, i, FEAT_AHEAD, slots):
                    features(0)
                    features(1)
                    if i >= 0:
                        values()
                if i >= 0:
                    act.wait_ge(yt_ready, n + 1)
                    nc.scalar.copy(yT[:, :, :], VY[:, GW:2 * GW]).then_inc(yt_done, 1)

            def after(g):
                pass

            def between(i):
                for u in ROUTER.get(i, ()):
                    act.wait_ge(rh_ready, u + 1)
                    nc.scalar.activation(hr[0:R, u * TU:(u + 1) * TU], router_bank[u][0:R, :], ACT.Relu,
                                         bias=br1_c[:, :]).then_inc(rh_done, 1)
                if i == WEIGHTS_STEP:
                    act.wait_ge(wt_ready, 1)
                    nc.scalar.copy(wtokT[:, :], KTOK[:, 0:P])
                    nc.scalar.copy(s1_b[:, :], KTOK[:, P:P + IB]).then_inc(wt_done, 1)
                if i == 1:
                    act.wait_ge(lgs_done, 1)
                    nc.scalar.activation(gate[:, :, :], gate[:, :, :], ACT.Exp).then_inc(ex_done, 1)
                if i == 3:
                    act.wait_ge(d_done, 1)
                    nc.scalar.activation(row2[:, :], row2[:, :], ACT.Exp, scale=0.5).then_inc(e2x_done, 1)

            group_0(step, after, between)
            act.wait_ge(wt_done, 1)
            for u in range(NU):
                for b in range(IB):
                    act.wait_ge(h_ready, u * IB + b + 1)
                    nc.scalar.activation(hid[:, u % 2, b, :], bank[b][:, :], ACT.Silu,
                                         bias=s1_b[:, b:b + 1]).then_inc(h_done, 1)

            def turn(s, k, r):
                if within(s, 0):
                    act.wait_ge(ht_ready, s + 1)
                    for half in range(2):
                        b = slice(half * IB // 2, (half + 1) * IB // 2)
                        nc.scalar.copy(hT_tile[:, b, :], bank[4][:, b.start * P:b.stop * P]).then_inc(ht_done, 1)
                if within(s, X_AHEAD):
                    act.wait_ge(t_ready, s + (X_AHEAD + 1))
                    nc.scalar.copy(xg_hi[:, k, :], bank[3][:, 0:P]).then_inc(t_hi, 1)
                if within(s, L1_AHEAD):
                    kk = (k + L1_AHEAD) % RING
                    act.wait_ge(l1_biased, s + (L1_AHEAD + 1))
                    nc.scalar.activation(h_tile[:, kk, :], h_tile[:, kk, :], ACT.Silu).then_inc(l1_done, 1)

            over_tiles(act, turn, lambda: None, lambda: None)
            slot_kept(step)

            def gate_steps(i):
                for u in GATES.get(i, ()):
                    act.wait_ge(combined, (u + 1) * UNIT)
                    part = slice(u * UNIT, (u + 1) * UNIT)
                    nc.scalar.activation(acc[:, part, :], acc[:, part, :], ACT.Silu).then_inc(g_done, 1)

            other_groups(act, step, after, gate_steps, lambda: None)

        @block.vector
        def _(vec):
            chain = [0]

            def link(ins):
                chain[0] += 1
                ins.then_inc(dve, 1)
                vec.wait_ge(dve, chain[0])

            nc.vector.memset(wf_raw[HD:P, 0, :], -0.5)
            nc.vector.memset(wf_raw[0:HD, 1, :], -0.5)
            nc.vector.memset(hr[R:R + 1, :], 1.0).then_inc(half_done, 1)
            def moments(u):
                vec.wait_ge(x_in[u], 16)
                for n in range(u * UNIT, (u + 1) * UNIT):
                    last = nc.vector.bn_stats(stats[:, n, :], x_sb[:, n, :])
                link(last)
                for n in range(u * UNIT, (u + 1) * UNIT):
                    last = nc.vector.bn_aggr(mean_var[:, n, :], stats[:, n, :])
                last.then_inc(var_done, 1)

            def scale(u):
                part = slice(u * UNIT, (u + 1) * UNIT)
                vec.wait_ge(pow_done, u + 1)
                nc.vector.scalar_tensor_tensor(minus_mean[:, part], mean_var[:, part, 0], -1.0, rstd[:, part],
                                               ALU.mult, ALU.mult).then_inc(rstd_done, 1)
                for n in range(u * UNIT, u * UNIT + UNIT // 2):
                    last = nc.vector.tensor_scalar(xn[:, n, :], x_sb[:, n, :], mean_var[:, n, 0:1], rstd[:, n:n + 1],
                                                   ALU.subtract, ALU.mult)
                last.then_inc(xn_done, 1)

            def low_part(u):
                vec.wait_ge(xhi_done, u + 1)
                t = slice(u * TU, (u + 1) * TU)
                nc.vector.tensor_tensor(xT_lo[:, t], bank[u][:, :], xT_hi[:, t].bitcast(F32),
                                        ALU.subtract).then_inc(xlo_done, 1)

            moments(0)
            moments(1)
            scale(0)
            moments(2)
            scale(1)
            moments(3)
            low_part(0)
            scale(2)
            scale(3)
            vec.wait_ge(w_hi_done[0], 1)
            nc.vector.tensor_tensor(w_lo[:, 0, :], w_raw[:, 0, :], w_hi[:, 0, :].bitcast(F32),
                                    ALU.subtract).then_inc(w_split[0], 1)
            for u in range(1, NU):
                low_part(u)
            vec.wait_ge(wf_in, 32)
            nc.vector.tensor_copy(wf_hi[:, :, :], wf_raw[:, :, :]).then_inc(wf_high, 1)
            vec.wait_ge(wf_high, 1)
            nc.vector.tensor_tensor(wf_lo[:, :, :], wf_raw[:, :, :], wf_hi[:, :, :].bitcast(F32),
                                    ALU.subtract).then_inc(wf_split, 1)
            for j in range(1, 3):
                vec.wait_ge(w_hi_done[j], 1)
                nc.vector.tensor_tensor(w_lo[:, j, :], w_raw[:, j, :], w_hi[:, j, :].bitcast(F32),
                                        ALU.subtract).then_inc(w_split[j], 1)

            def step(g, i, slots):
                n = g * NCHUNK + i
                if i in RESPLIT and (not isinstance(g, int) or g == 0):
                    j = RESPLIT[i][0]
                    vec.wait_ge(w_hi_done[j], g + 2)
                    nc.vector.tensor_tensor(w_lo[:, j, :], w_raw[:, j, :], w_hi[:, j, :].bitcast(F32),
                                            ALU.subtract).then_inc(w_split[j], 1)
                if i >= 0:
                    vec.wait_ge(score_ready, n + 1)
                    nc.vector.tensor_tensor(probs[:, :, :], SCORE[:, :].rearrange("p (h q) -> p h q", q=P),
                                            causal[:, :].unsqueeze(1).to_broadcast([P, HG, P]), ALU.mult).then_inc(masked, 1)
                def stack_q():
                    s = (i + PROJ_AHEAD) % 2
                    if i < 0:
                        vec.wait_ge(squared, n + PROJ_AHEAD + 1)
                        for rows, h in HEADS:
                            last = nc.vector.tensor_copy(stack_hi[rows, s, h, :], proj_bank(i)[rows, :])
                        last.then_inc(q_high, 1)
                    vec.wait_ge(q_high, n + PROJ_AHEAD + 1)
                    for rows, h in HEADS:
                        last = nc.vector.tensor_tensor(stack_lo[rows, s, h, :], proj_bank(i)[rows, :],
                                                       stack_hi[rows, s, h, :].bitcast(F32), ALU.subtract)
                    last.then_inc(q_low, 1)

                if i < 0 and ahead(g, i, PROJ_AHEAD, slots):
                    stack_q()
                    s = (i + PROJ_AHEAD) % 2
                    vec.wait_ge(sq_high, (n + PROJ_AHEAD + 1) * 2)
                    nc.vector.tensor_tensor(stack_lo[0:HD, s, 1, :], squares[0:HD, s, :],
                                            stack_hi[0:HD, s, 1, :].bitcast(F32), ALU.subtract).then_inc(sq_low[1], 1)
                if i >= 0:
                    vec.wait_ge(outp_ready, n + 1)
                    o = OUT[:, 0:HG * EV].rearrange("p (h e) -> p h e", e=EV)
                    nc.vector.tensor_scalar(den[:, :], o[:, :, HD], NF * EPS, None, ALU.add).then_inc(den_done, 1)
                    vec.wait_ge(den_done, n * 2 + 1)
                    nc.vector.reciprocal(den[:, :], den[:, :]).then_inc(den_done, 1)
                    vec.wait_ge(den_done, n * 2 + 2)
                    nc.vector.tensor_tensor(y[:, :, :], o[:, :, 0:HD], den[:, :].unsqueeze(2).to_broadcast([P, HG, HD]),
                                            ALU.mult).then_inc(y_done, 1)
                    if ahead(g, i, PROJ_AHEAD, slots):
                        stack_q()
                    vec.wait_ge(st_ready, g * (NCHUNK + 1) + (i + 1))
                    if i > 0:
                        gather(i - 1, STATE)
                    if i < NCHUNK - 1:
                        new, old = state[:, (i + 1) % 2, :, :], state[:, i % 2, :, :]
                        delta = STATE[:, 0:HG * EV].rearrange("p (h e) -> p h e", e=EV)
                        if i == 0:
                            nc.vector.tensor_copy(new, delta).then_inc(st_done, 1)
                        else:
                            vec.wait_ge(st_done, g * (NCHUNK - 1) + i)
                            nc.vector.tensor_tensor(new, delta, old, ALU.add).then_inc(st_done, 1)

            def gather(i, src):
                nc.vector.tensor_tensor(s_sum[:, i, :], src[:, 384:384 + C], s_sum[:, i, :], ALU.add).then_inc(s_added, 1)

            def after(g):
                vec.wait_ge(st_ready, g * (NCHUNK + 1) + (NCHUNK + 1))
                gather(NCHUNK - 1, OUT)

            def bc(a, k=E):
                return a.unsqueeze(2).to_broadcast([P, NCHUNK, k])

            def between(i):
                if i == 0:
                    vec.wait_ge(consts_done, 6)
                if i == -1:
                    vec.wait_ge(lg_ready, 1)
                    nc.vector.tensor_copy(gate[:, :, :], OUT[:, 0:NCHUNK * E]).then_inc(lg_done, 1)
                if i == 0:
                    vec.wait_ge(lg_done, 1)
                    link(nc.vector.tensor_reduce(row1[:, :], gate[:, :, :], AX.X, ALU.max))
                    nc.vector.tensor_tensor(gate[:, :, :], gate[:, :, :], bc(row1[:, :]), ALU.subtract).then_inc(lgs_done, 1)
                if i == 2:
                    vec.wait_ge(ex_done, 1)
                    link(nc.vector.tensor_reduce(row1[:, :], gate[:, :, :], AX.X, ALU.add))
                    link(nc.vector.reciprocal(row1[:, :], row1[:, :]))
                    link(nc.vector.tensor_tensor(gate[:, :, :], gate[:, :, :], bc(row1[:, :]), ALU.mult))
                    for n in range(NCHUNK):
                        last = nc.vector.max(top[:, n, :], gate[:, n, :])
                    link(last)
                    nc.vector.tensor_tensor(row2[:, :], top[:, :, 1], top[:, :, 0], ALU.subtract).then_inc(d_done, 1)
                if i == 3:
                    for n in range(NCHUNK):
                        last = nc.vector.max_index(top_at[:, n, :], top[:, n, :], gate[:, n, :])
                    link(last)
                    link(nc.vector.tensor_copy(top_e[:, :, :], top_at[:, :, 0:2]))
                if i == 4:
                    vec.wait_ge(e2x_done, 1)
                    link(nc.vector.tensor_scalar(row1[:, :], row2[:, :], 1.0, None, ALU.add))
                    link(nc.vector.reciprocal(tp[:, 0, :], row1[:, :]))
                    nc.vector.tensor_tensor(tp[:, 1, :], tp[:, 0, :], row2[:, :], ALU.mult)
                    for k in range(TOP):
                        last = nc.vector.tensor_tensor(chosen[:, k, :, :], iota_e[:, :, :], bc(top_e[:, :, k]), ALU.is_equal)
                    link(last)
                    nc.vector.tensor_tensor(wtmp[:, :, :], chosen[:, 0, :, :], chosen[:, 1, :, :], ALU.add).then_inc(chosen_done, 1)
                if i == RANK_STEP:
                    vec.wait_ge(rank_ready, 1)
                    nc.vector.tensor_copy(ranks[:, :, :, :], KTOK[:, 0:2 * P]).then_inc(rank_done, 1)
                    vec.wait_ge(rank_done, 1)
                    for e in range(E):
                        last = nc.vector.tensor_tensor_scan(upto[:, :, e], ones[:, 0:NCHUNK], ranks[:, 1, :, e], 0.0,
                                                            ALU.mult, ALU.add)
                    link(last)
                    link(nc.vector.tensor_scalar(count_i[:, :], upto[:, NCHUNK - 1, :], float(P - 1), None, ALU.add))
                    link(nc.vector.tensor_scalar(count_i[:, :], count_i[:, :], SHIFT, None, ALU.arith_shift_right))
                    link(nc.vector.tensor_copy(tiles_of[:, :], count_i[:, :]))
                    link(nc.vector.tensor_tensor_scan(tile_end[:, :], ones[:, 0:E], tiles_of[:, :], 0.0, ALU.mult, ALU.add))
                if i == RANK_STEP + 1:
                    link(nc.vector.tensor_tensor(slot_base[:, :], tile_end[:, :], tiles_of[:, :], ALU.subtract))
                    link(nc.vector.tensor_scalar(slot_base[:, :], slot_base[:, :], float(P), None, ALU.mult))
                    link(nc.vector.tensor_tensor(upto[:, :, :], upto[:, :, :], ranks[:, 1, :, :], ALU.subtract))
                    link(nc.vector.tensor_tensor(upto[:, :, :], upto[:, :, :], ranks[:, 0, :, :], ALU.add))
                    link(nc.vector.tensor_tensor(upto[:, :, :], upto[:, :, :],
                                                 slot_base[:, :].unsqueeze(1).to_broadcast([P, NCHUNK, E]), ALU.add))
                if i == RANK_STEP + 2:
                    for k in range(TOP):
                        link(nc.vector.tensor_tensor(wtmp[:, :, :], upto[:, :, :], chosen[:, k, :, :], ALU.mult))
                        link(nc.vector.tensor_reduce(slot_f[:, k, :], wtmp[:, :, :], AX.X, ALU.add))
                    nc.vector.tensor_copy(slot[:, :, :], slot_f[:, :, :]).then_inc(slots_done, 1)
                if i == RANK_STEP + 3:
                    link(nc.vector.tensor_tensor(iota_t[:, :, :], iota_t[:, :, :],
                                                 tile_end[:, 0:E - 1].unsqueeze(1).to_broadcast([P, TILES, E - 1]), ALU.is_ge))
                    link(nc.vector.tensor_reduce(expert_f[:, :], iota_t[:, :, :], AX.X, ALU.add))
                    nc.vector.tensor_copy(expert[:, :], expert_f[:, :]).then_inc(experts_done, 1)
                    for k in range(TOP):
                        last = nc.vector.tensor_tensor(chosen[:, k, :, :], chosen[:, k, :, :], bc(tp[:, k, :]), ALU.mult)
                    link(last)
                    nc.vector.tensor_tensor(wtok[:, :, :], chosen[:, 0, :, :], chosen[:, 1, :, :], ALU.add).then_inc(w_done, 1)

            vec.wait_ge(consts_done, 5)
            group_0(step, after, between)
            vec.wait_ge(feat_ready, 2 * KEPT)
            for e in range(EARLY, E + 1):
                vec.wait_ge(e1_in[e % 2], 16 * (e // 2 + 1))
                link(nc.vector.tensor_copy(e1_hi[:, e, :], e1_raw[:, e % 2, :]))
                nc.vector.tensor_tensor(e1_lo[:, e, :], e1_raw[:, e % 2, :], e1_hi[:, e, :].bitcast(F32),
                                        ALU.subtract).then_inc(late_split, 1)

            vec.wait_ge(b_in, 32)

            def expert_sum(u):
                vec.wait_ge(scattered[u], 16 * TOP * UNIT)
                vec.wait_ge(o_ready, u + 1)
                nc.vector.tensor_tensor(acc[:, u * UNIT:(u + 1) * UNIT, :],
                                        bank[4 + u % 2][:, :].rearrange("p (n c) -> p n c", c=C),
                                        bs2_b[:, :].unsqueeze(1).to_broadcast([P, UNIT, C]), ALU.add).then_inc(o_done, 1)

            for u in range(NU - 1):
                expert_sum(u)
            vec.wait_ge(experts_done, 1)
            vec.wait_ge(e1b_in, 16)

            def turn(s, k, r):
                if within(s, L1_AHEAD):
                    kk = (k + L1_AHEAD) % RING
                    of = nc.vector.value_load(expert[0:1, bass.ds(s + L1_AHEAD, 1)], min_val=0, max_val=E - 1)
                    vec.wait_ge(l1_ready, s + (L1_AHEAD + 1))
                    nc.vector.tensor_tensor(h_tile[:, kk, :], bank[kk][:, :], e1_b[:, bass.ds(of, 1), :], ALU.add).then_inc(l1_biased, 1)
                if within(s, X_AHEAD):
                    vec.wait_ge(t_hi, s + (X_AHEAD + 1))
                    nc.vector.tensor_tensor(xg_lo[:, k, :], bank[3][:, 0:P], xg_hi[:, k, :].bitcast(F32),
                                            ALU.subtract).then_inc(t_lo, 1)
                if within(s, 0):
                    vec.wait_ge(l2_ready, s + 1)
                    if not isinstance(s, int) or s >= RING:
                        vec.wait_ge(stored[k], r * 16)
                    nc.vector.tensor_copy(y_ring[:, k, :], bank[5 + k][:, 0:C]).then_inc(l2_done, 1)

            over_tiles(vec, turn, lambda: expert_sum(NU - 1), lambda: None)
            slot_kept(step)

            def finish(j):
                first, upto = DVE_PARTS[j]
                part = slice(first, upto)
                vec.wait_ge(s_added, (NG - 1) * NCHUNK + upto)
                nc.vector.tensor_tensor(s_sum[:, part, :], s_sum[:, part, :], acc[:, part, :], ALU.mult).then_inc(m_done, 1)
                vec.wait_ge(m_done, j + 1)
                nc.vector.tensor_tensor(x_sb[:, part, :], x_sb[:, part, :], s_sum[:, part, :], ALU.add).then_inc(res_done, 1)

            def combine(i):
                for n in GATHERS.get(i - 1, ()):
                    vec.wait_ge(gathered[n % 4], 16 * TOP * (n // 4 + 1))
                    link(nc.vector.scalar_tensor_tensor(acc[:, n, :], got[:, n % 4, 0, :], tp[:, 0, n:n + 1],
                                                        acc[:, n, :], ALU.mult, ALU.add))
                    nc.vector.scalar_tensor_tensor(acc[:, n, :], got[:, n % 4, 1, :], tp[:, 1, n:n + 1],
                                                   acc[:, n, :], ALU.mult, ALU.add).then_inc(combined, 1)
                if i == NCHUNK - 1:
                    vec.wait_ge(g_done, NU)
                    finish(0)

            other_groups(vec, step, after, combine, lambda: None)
            finish(1)


NAMES = ['L0_attn_x', 'L0_attn_Wq', 'L0_attn_Wk', 'L0_attn_Wv', 'L0_attn_Wo', 'L0_attn_W_feat',
         'L0_ffn_Wr1', 'L0_ffn_br1', 'L0_ffn_Wr2', 'L0_ffn_br2', 'L0_ffn_Ws1', 'L0_ffn_bs1', 'L0_ffn_Ws2',
         'L0_ffn_bs2', 'L0_ffn_We1', 'L0_ffn_be1', 'L0_ffn_We2', 'L0_ffn_be2']


def kernel(**inputs):
    import numpy as np
    import concourse.bacc as bacc
    from concourse.bass_utils import run_bass_kernel_spmd

    nc = bacc.Bacc("TRN2", target_bir_lowering=False, num_devices=1)
    arrays, args = {}, []
    for name in NAMES:
        a = np.ascontiguousarray(inputs[name])
        arrays[name] = a
        args.append(nc.dram_tensor(name, a.shape, mybir.dt.from_np(a.dtype), kind="ExternalInput").ap())
    shape = arrays['L0_attn_x'].shape
    out = nc.dram_tensor("out", shape, F32, kind="ExternalOutput").ap()
    build(nc, *args, out)
    return run_bass_kernel_spmd(nc, [arrays], core_ids=[0]).results[0]["out"]
```
